# Optimizing a Trainium2 kernel written in Bass

```python
import numpy as np
import jax
import jax.numpy as jnp

def _softmax(x, axis=-1):
    return jax.nn.softmax(x, axis=axis)

def _gelu(x):
    return jax.nn.gelu(x, approximate=True)

def _silu(x):
    return jax.nn.silu(x)

def _sigmoid(x):
    return jax.nn.sigmoid(x)

def _layernorm(x, axis=-1, eps=1e-05):
    m = jnp.mean(x, axis=axis, keepdims=True)
    v = jnp.var(x, axis=axis, keepdims=True)
    return (x - m) / jnp.sqrt(v + eps)

def _scatter_add(tgt, idx, src, axis=0):
    return tgt.at[idx].add(src)

def _segment_sum(src, seg, n):
    return jax.ops.segment_sum(src, seg, n)
kernel_name = 'mk_hybrid_d1_jaxref_r8_7b8462'

def setup_inputs(seed: int=0):
    np.random.seed(seed)
    _w = jnp.asarray

    def _L0_attn_a_setup():
        import jax, jax.numpy as jnp
        import numpy as np
        HEADS = 16
        DIM_HEADS = 64
        NUM_BUCKETS = 32
        MAX_DISTANCE = 128

        def _relative_position_bucket(rel_pos, num_buckets=NUM_BUCKETS, max_distance=MAX_DISTANCE):
            n = jnp.maximum(-rel_pos, 0)
            max_exact = num_buckets // 2
            is_small = n < max_exact
            nf = jnp.maximum(n, 1).astype(jnp.float32)
            val_if_large = max_exact + (jnp.log(nf / max_exact) / np.log(max_distance / max_exact) * (num_buckets - max_exact)).astype(jnp.int32)
            val_if_large = jnp.minimum(val_if_large, num_buckets - 1)
            return jnp.where(is_small, n, val_if_large)
        key = jax.random.key(seed)
        ks = jax.random.split(key, 6)
        B, N, D = (2, 256, 128)
        inner = HEADS * DIM_HEADS
        x = jax.random.normal(ks[0], (B, N, D), dtype=jnp.float32)
        Wq = jax.random.normal(ks[1], (D, inner), dtype=jnp.float32) * 0.02
        Wkv = jax.random.normal(ks[2], (D, 2 * DIM_HEADS), dtype=jnp.float32) * 0.02
        Wout = jax.random.normal(ks[3], (inner, D), dtype=jnp.float32) * 0.02
        bout = jnp.zeros((D,), dtype=jnp.float32)
        rel_emb = jax.random.normal(ks[4], (NUM_BUCKETS, HEADS), dtype=jnp.float32) * 0.02
        return {'x': x, 'Wq': Wq, 'Wkv': Wkv, 'Wout': Wout, 'bout': bout, 'rel_emb': rel_emb}
    _L0_attn_a_in = _L0_attn_a_setup()

    def _L0_attn_b_setup():
        import jax, jax.numpy as jnp
        import numpy as np
        B, T, D, H, PD = (1, 256, 128, 16, 4)
        DH = D // H
        SCALE = DH ** (-0.5)
        _PI = jnp.array([0, 0, 0, 1, 1, 2])
        _PJ = jnp.array([1, 2, 3, 2, 3, 3])
        J6 = jnp.array([[0, 0, 0, 0, 0, 1], [0, 0, 0, 0, -1, 0], [0, 0, 0, 1, 0, 0], [0, 0, 1, 0, 0, 0], [0, -1, 0, 0, 0, 0], [1, 0, 0, 0, 0, 0]], dtype=jnp.float32)

        def exterior(p1, p2):
            L = p1[..., _PI] * p2[..., _PJ] - p1[..., _PJ] * p2[..., _PI]
            n = jnp.clip(jnp.linalg.norm(L, axis=-1, keepdims=True), 1e-12)
            return L / n
        key = jax.random.key(seed)
        ks = jax.random.split(key, 10)
        s = 0.02
        return {'x': jax.random.normal(ks[0], (B, T, D), dtype=jnp.float32), 'qkv_w': jax.random.normal(ks[1], (D, 3 * D), dtype=jnp.float32) * s, 'qkv_b': jnp.zeros((3 * D,), dtype=jnp.float32), 'w1_write': jax.random.normal(ks[2], (D, PD * H), dtype=jnp.float32) * s, 'w2_write': jax.random.normal(ks[3], (D, PD * H), dtype=jnp.float32) * s, 'w1_read': jax.random.normal(ks[4], (D, PD * H), dtype=jnp.float32) * s, 'w2_read': jax.random.normal(ks[5], (D, PD * H), dtype=jnp.float32) * s, 'kv_geo_w': jax.random.normal(ks[6], (D, 2 * D), dtype=jnp.float32) * s, 'out_w': jax.random.normal(ks[7], (D, D), dtype=jnp.float32) * s, 'out_b': jnp.zeros((D,), dtype=jnp.float32), 'kv_gate': jnp.asarray(0.01, dtype=jnp.float32), 'mem_scale': jnp.full((H,), 0.1, dtype=jnp.float32), 'decay_logits': jnp.full((H,), 4.6, dtype=jnp.float32)}
    _L0_attn_b_in = _L0_attn_b_setup()

    def _L0_ffn_setup():
        import jax, jax.numpy as jnp
        import numpy as np
        MIN_EXPERT_CAPACITY = 4
        CAPACITY_FACTOR = 1.0

        def _moe_forward(x, router_w, w1, b1, w2, b2):
            B, S, D = x.shape
            E = router_w.shape[1]
            G = 1
            T = B * S
            C = max(int(round(CAPACITY_FACTOR * T / E)), MIN_EXPERT_CAPACITY)
            xt = x.reshape(G, T, D)
            logits = jnp.einsum('gtd,de->gte', xt, router_w)
            probs = jax.nn.softmax(logits, axis=-1)
            gate = jnp.max(probs, axis=-1)
            idx = jnp.argmax(probs, axis=-1)
            emask = jax.nn.one_hot(idx, E, dtype=x.dtype)
            pos = jnp.cumsum(emask, axis=1) * emask - 1.0
            pos = pos.astype(jnp.int32)
            slot = jax.nn.one_hot(pos, C, dtype=x.dtype)
            dispatch = emask[..., None] * slot
            combine = dispatch * gate[..., None, None]
            expert_inputs = jnp.einsum('gtd,gtec->gecd', xt, dispatch)
            h = jax.nn.relu(jnp.einsum('gecd,edf->gecf', expert_inputs, w1) + b1[None, :, None, :])
            expert_outputs = jnp.einsum('gecf,efd->gecd', h, w2) + b2[None, :, None, :]
            out = jnp.einsum('gecd,gtec->gtd', expert_outputs, combine)
            return out.reshape(B, S, D)
        key = jax.random.key(seed)
        k0, k1, k2, k3 = jax.random.split(key, 4)
        B, S, D, E, F = (4, 256, 128, 8, 512)
        x = jax.random.normal(k0, (B, S, D), dtype=jnp.float32)
        router_w = jax.random.normal(k1, (D, E), dtype=jnp.float32) * D ** (-0.5)
        w1 = jax.random.normal(k2, (E, D, F), dtype=jnp.float32) * D ** (-0.5)
        b1 = jnp.zeros((E, F), dtype=jnp.float32)
        w2 = jax.random.normal(k3, (E, F, D), dtype=jnp.float32) * F ** (-0.5)
        b2 = jnp.zeros((E, D), dtype=jnp.float32)
        return {'x': x, 'router_w': router_w, 'w1': w1, 'b1': b1, 'w2': w2, 'b2': b2}
    _L0_ffn_in = _L0_ffn_setup()
    _d = {'L0_attn_a_x': _L0_attn_a_in['x'], 'L0_attn_a_Wq': _L0_attn_a_in['Wq'], 'L0_attn_a_Wkv': _L0_attn_a_in['Wkv'], 'L0_attn_a_Wout': _L0_attn_a_in['Wout'], 'L0_attn_a_bout': _L0_attn_a_in['bout'], 'L0_attn_a_rel_emb': _L0_attn_a_in['rel_emb'], 'L0_attn_b_qkv_w': _L0_attn_b_in['qkv_w'], 'L0_attn_b_qkv_b': _L0_attn_b_in['qkv_b'], 'L0_attn_b_w1_write': _L0_attn_b_in['w1_write'], 'L0_attn_b_w2_write': _L0_attn_b_in['w2_write'], 'L0_attn_b_w1_read': _L0_attn_b_in['w1_read'], 'L0_attn_b_w2_read': _L0_attn_b_in['w2_read'], 'L0_attn_b_kv_geo_w': _L0_attn_b_in['kv_geo_w'], 'L0_attn_b_out_w': _L0_attn_b_in['out_w'], 'L0_attn_b_out_b': _L0_attn_b_in['out_b'], 'L0_attn_b_kv_gate': _L0_attn_b_in['kv_gate'], 'L0_attn_b_mem_scale': _L0_attn_b_in['mem_scale'], 'L0_attn_b_decay_logits': _L0_attn_b_in['decay_logits'], 'L0_ffn_router_w': _L0_ffn_in['router_w'], 'L0_ffn_w1': _L0_ffn_in['w1'], 'L0_ffn_b1': _L0_ffn_in['b1'], 'L0_ffn_w2': _L0_ffn_in['w2'], 'L0_ffn_b2': _L0_ffn_in['b2']}
    _x0 = _d['L0_attn_a_x']
    _d['L0_attn_a_x'] = jax.random.normal(jax.random.fold_in(jax.random.key(seed), 1), (2, 1024, 128), dtype=_x0.dtype)
    del _x0
    return _d

def reference(L0_attn_a_x, L0_attn_a_Wq, L0_attn_a_Wkv, L0_attn_a_Wout, L0_attn_a_bout, L0_attn_a_rel_emb, L0_attn_b_qkv_w, L0_attn_b_qkv_b, L0_attn_b_w1_write, L0_attn_b_w2_write, L0_attn_b_w1_read, L0_attn_b_w2_read, L0_attn_b_kv_geo_w, L0_attn_b_out_w, L0_attn_b_out_b, L0_attn_b_kv_gate, L0_attn_b_mem_scale, L0_attn_b_decay_logits, L0_ffn_router_w, L0_ffn_w1, L0_ffn_b1, L0_ffn_w2, L0_ffn_b2):

    def _L0_attn_a_ref(x, Wq, Wkv, Wout, bout, rel_emb):
        import jax, jax.numpy as jnp
        import numpy as np
        HEADS = 16
        DIM_HEADS = 64
        NUM_BUCKETS = 32
        MAX_DISTANCE = 128

        def _relative_position_bucket(rel_pos, num_buckets=NUM_BUCKETS, max_distance=MAX_DISTANCE):
            n = jnp.maximum(-rel_pos, 0)
            max_exact = num_buckets // 2
            is_small = n < max_exact
            nf = jnp.maximum(n, 1).astype(jnp.float32)
            val_if_large = max_exact + (jnp.log(nf / max_exact) / np.log(max_distance / max_exact) * (num_buckets - max_exact)).astype(jnp.int32)
            val_if_large = jnp.minimum(val_if_large, num_buckets - 1)
            return jnp.where(is_small, n, val_if_large)
        B, N, D = x.shape
        h, dh = (HEADS, DIM_HEADS)
        scale = dh ** (-0.5)
        bias_scale = dh ** 0.5
        q = (x @ Wq).reshape(B, N, h, dh).transpose(0, 2, 1, 3) * scale
        kv = x @ Wkv
        k, v = (kv[..., :dh], kv[..., dh:])
        sim = jnp.einsum('bhid,bjd->bhij', q, k)
        pos = jnp.arange(N, dtype=jnp.int32)
        rel_pos = pos[None, :] - pos[:, None]
        rp_bucket = _relative_position_bucket(rel_pos)
        bias = rel_emb[rp_bucket]
        sim = sim + bias.transpose(2, 0, 1)[None] * bias_scale
        causal = jnp.triu(jnp.ones((N, N), dtype=bool), k=1)
        sim = jnp.where(causal[None, None], -jnp.finfo(sim.dtype).max, sim)
        attn = jax.nn.softmax(sim, axis=-1)
        out = jnp.einsum('bhij,bjd->bhid', attn, v)
        out = out.transpose(0, 2, 1, 3).reshape(B, N, h * dh)
        return out @ Wout + bout

    def _L0_attn_b_ref(x, qkv_w, qkv_b, w1_write, w2_write, w1_read, w2_read, kv_geo_w, out_w, out_b, kv_gate, mem_scale, decay_logits):
        import jax, jax.numpy as jnp
        import numpy as np
        B, T, D, H, PD = (1, 256, 128, 16, 4)
        DH = D // H
        SCALE = DH ** (-0.5)
        _PI = jnp.array([0, 0, 0, 1, 1, 2])
        _PJ = jnp.array([1, 2, 3, 2, 3, 3])
        J6 = jnp.array([[0, 0, 0, 0, 0, 1], [0, 0, 0, 0, -1, 0], [0, 0, 0, 1, 0, 0], [0, 0, 1, 0, 0, 0], [0, -1, 0, 0, 0, 0], [1, 0, 0, 0, 0, 0]], dtype=jnp.float32)

        def exterior(p1, p2):
            L = p1[..., _PI] * p2[..., _PJ] - p1[..., _PJ] * p2[..., _PI]
            n = jnp.clip(jnp.linalg.norm(L, axis=-1, keepdims=True), 1e-12)
            return L / n
        b, t, d = x.shape
        qkv = (x @ qkv_w + qkv_b).reshape(b, t, 3, H, DH)
        q = qkv[:, :, 0].transpose(0, 2, 1, 3)
        k = qkv[:, :, 1].transpose(0, 2, 1, 3)
        v = qkv[:, :, 2].transpose(0, 2, 1, 3)
        x_prev = jnp.concatenate([jnp.zeros((b, 1, d), x.dtype), x[:, :-1]], axis=1)
        w1 = (x_prev @ w1_write).reshape(b, t, H, PD)
        w2 = (x @ w2_write).reshape(b, t, H, PD)
        write_lines = exterior(w1, w2)
        r1 = (x @ w1_read).reshape(b, t, H, PD)
        r2 = (x @ w2_read).reshape(b, t, H, PD)
        read_lines = exterior(r1, r2)
        j_write = jnp.einsum('bthi,ij->bthj', write_lines, J6)
        incidence = jnp.einsum('bthp,bshp->bhts', read_lines, j_write)
        pos = jnp.arange(t)
        diffs = pos[:, None] - pos[None, :]
        causal = diffs > 0
        decays = jax.nn.sigmoid(decay_logits)
        expn = jnp.maximum(diffs, 0).astype(x.dtype)
        weights = jnp.where(causal[None], decays[:, None, None] ** expn[None], 0.0)
        mem_score = jnp.einsum('bhts,hts->bht', incidence ** 2, weights)
        gram_gate = jax.nn.sigmoid(mem_score * mem_scale[None, :, None])[..., None]
        kv_geo = (x @ kv_geo_w).reshape(b, t, 2, H, DH)
        k_geo = kv_geo[:, :, 0].transpose(0, 2, 1, 3)
        v_geo = kv_geo[:, :, 1].transpose(0, 2, 1, 3)
        k_enh = k + kv_gate * gram_gate * k_geo
        v_enh = v + kv_gate * gram_gate * v_geo
        scores = jnp.einsum('bhtd,bhsd->bhts', q, k_enh) * SCALE
        scores = jnp.where((diffs >= 0)[None, None], scores, -jnp.inf)
        attn = jax.nn.softmax(scores, axis=-1)
        out = jnp.einsum('bhts,bhsd->bhtd', attn, v_enh)
        out = out.transpose(0, 2, 1, 3).reshape(b, t, d)
        return out @ out_w + out_b

    def _L0_ffn_ref(x, router_w, w1, b1, w2, b2):
        import jax, jax.numpy as jnp
        import numpy as np
        MIN_EXPERT_CAPACITY = 4
        CAPACITY_FACTOR = 1.0

        def _moe_forward(x, router_w, w1, b1, w2, b2):
            B, S, D = x.shape
            E = router_w.shape[1]
            G = 1
            T = B * S
            C = max(int(round(CAPACITY_FACTOR * T / E)), MIN_EXPERT_CAPACITY)
            xt = x.reshape(G, T, D)
            logits = jnp.einsum('gtd,de->gte', xt, router_w)
            probs = jax.nn.softmax(logits, axis=-1)
            gate = jnp.max(probs, axis=-1)
            idx = jnp.argmax(probs, axis=-1)
            emask = jax.nn.one_hot(idx, E, dtype=x.dtype)
            pos = jnp.cumsum(emask, axis=1) * emask - 1.0
            pos = pos.astype(jnp.int32)
            slot = jax.nn.one_hot(pos, C, dtype=x.dtype)
            dispatch = emask[..., None] * slot
            combine = dispatch * gate[..., None, None]
            expert_inputs = jnp.einsum('gtd,gtec->gecd', xt, dispatch)
            h = jax.nn.relu(jnp.einsum('gecd,edf->gecf', expert_inputs, w1) + b1[None, :, None, :])
            expert_outputs = jnp.einsum('gecf,efd->gecd', h, w2) + b2[None, :, None, :]
            out = jnp.einsum('gecd,gtec->gtd', expert_outputs, combine)
            return out.reshape(B, S, D)
        return _moe_forward(x, router_w, w1, b1, w2, b2)
    x = L0_attn_a_x
    x = x + _L0_attn_a_ref(_layernorm(x, axis=-1), L0_attn_a_Wq, L0_attn_a_Wkv, L0_attn_a_Wout, L0_attn_a_bout, L0_attn_a_rel_emb)
    x = x + _L0_ffn_ref(_layernorm(x, axis=-1), L0_ffn_router_w, L0_ffn_w1, L0_ffn_b1, L0_ffn_w2, L0_ffn_b2)
    x = x + _L0_attn_b_ref(_layernorm(x, axis=-1), L0_attn_b_qkv_w, L0_attn_b_qkv_b, L0_attn_b_w1_write, L0_attn_b_w2_write, L0_attn_b_w1_read, L0_attn_b_w2_read, L0_attn_b_kv_geo_w, L0_attn_b_out_w, L0_attn_b_out_b, L0_attn_b_kv_gate, L0_attn_b_mem_scale, L0_attn_b_decay_logits)
    x = x + _L0_ffn_ref(_layernorm(x, axis=-1), L0_ffn_router_w, L0_ffn_w1, L0_ffn_b1, L0_ffn_w2, L0_ffn_b2)
    return x

_drawn_inputs = setup_inputs


def setup_inputs(seed=0):
    import zlib

    import numpy as np

    out = dict(_drawn_inputs(seed))
    spreads = {'L0_attn_a_bout': (0.0, 0.1),
     'L0_attn_b_qkv_b': (0.0, 0.1),
     'L0_attn_b_out_b': (0.0, 0.1),
     'L0_attn_b_mem_scale': (0.10000000149011612, 0.6),
     'L0_attn_b_decay_logits': (4.599999904632568, 0.6),
     'L0_ffn_b1': (0.0, 0.1),
     'L0_ffn_b2': (0.0, 0.1)}
    factors = {'L0_attn_a_Wq': 5.687,
     'L0_attn_a_rel_emb': 3.521,
     'L0_attn_b_w1_write': 200.0,
     'L0_attn_b_w2_write': 200.0,
     'L0_attn_b_w1_read': 200.0,
     'L0_attn_b_w2_read': 200.0,
     'L0_attn_b_kv_geo_w': 158.49}
    for name, (base, spread) in spreads.items():
        noise = np.random.default_rng([zlib.crc32(name.encode()), seed]).standard_normal(out[name].shape)
        drawn = base * np.exp(spread * noise) if base else spread * noise
        out[name] = jnp.asarray(drawn.astype(out[name].dtype))
    for name, factor in factors.items():
        out[name] = (out[name] * factor).astype(out[name].dtype)
    return out
```

```python
import numpy as np
import concourse.bass as bass
from concourse import mybir
from contextlib import ExitStack

F32 = mybir.dt.float32
F32R = mybir.dt.float32r
BF16 = mybir.dt.bfloat16
I32 = mybir.dt.int32
ALU = mybir.AluOpType
ACT = mybir.ActivationFunctionType
AX = mybir.AxisListType

P = 128
BATCH, SEQ, D = 2, 1024, 128
TOK = BATCH * SEQ
TILES = TOK // P
QT = SEQ // P
BANK = 512
BLK = BANK // P
EPS = 1e-5
MASKED = 1e30

A_HEADS, A_DH = 16, 64
BUCKETS, MAX_DIST = 32, 128
BIAS_W = 2 * P
BIAS_M = P + BIAS_W - 1
B_HEADS, B_DH = 16, 8
GRP = 4
REP = P // (GRP * B_DH)
PAIRS = 21
ROWS = 7 * B_HEADS
E, F, CAP = 8, 512, TOK // 8
FB = F // P
SLOTS = E * CAP


class Chain:

    def __init__(self, eng, sem):
        self.eng, self.sem, self.n = eng, sem, 0

    def __call__(self, ins):
        self.n += 1
        ins.then_inc(self.sem, 1)
        self.eng.wait_ge(self.sem, self.n)


class Phase:

    def __init__(self, nc, name):
        self.nc, self.name = nc, name

    def __enter__(self):
        self.ctx = ExitStack()
        return self

    def sem(self, name):
        return self.ctx.enter_context(self.nc.semaphore(f"{self.name}_{name}"))

    def psum(self, name, shape):
        return self.ctx.enter_context(self.nc.psum_tensor(f"{self.name}_{name}", shape, F32))

    def sb(self, name, shape, dt=F32):
        return self.ctx.enter_context(self.nc.sbuf_tensor(f"{self.name}_{name}", shape, dt))

    def block(self):
        return self.ctx.enter_context(self.nc.Block())

    def __exit__(self, *a):
        return self.ctx.__exit__(*a)


def layernorm(nc, name, X, xn, xnT, ident):
    with Phase(nc, name) as ph:
        stats, mv = ph.sb("stats", [P, TILES, 6]), ph.sb("mv", [P, TILES, 2])
        var, dev, rstd = ph.sb("var", [P, TILES]), ph.sb("dev", [P, TILES]), ph.sb("rstd", [P, TILES])
        bank = [ph.psum(f"bank{i}", [P, BANK]) for i in range(TILES // BLK)]
        chain, var_ready, dev_ready = ph.sem("chain"), ph.sem("var_ready"), ph.sem("dev_ready")
        xn_ready, turned, copied = ph.sem("xn_ready"), ph.sem("turned"), ph.sem("copied")
        block = ph.block()

        @block.vector
        def _(dve):
            link = Chain(dve, chain)
            nc.vector.memset(xnT[:, :, 0:1], 0.0)
            for i in range(TILES):
                ins = nc.vector.bn_stats(stats[:, i, :], X[:, i, :])
            link(ins)
            for i in range(TILES):
                ins = nc.vector.bn_aggr(mv[:, i, :], stats[:, i, :])
            link(ins)
            nc.vector.tensor_scalar(var[:, :], mv[:, :, 1], EPS, None, ALU.add).then_inc(var_ready, 1)
            dve.wait_ge(dev_ready, 1)
            link(nc.vector.reciprocal(rstd[:, :], dev[:, :]))
            for i in range(TILES):
                nc.vector.tensor_scalar(xn[:, i, :], X[:, i, :], mv[:, i, 0:1], rstd[:, i:i + 1],
                                        ALU.subtract, ALU.mult).then_inc(xn_ready, 1)

        @block.scalar
        def _(act):
            act.wait_ge(var_ready, 1)
            nc.scalar.activation(dev[:, :], var[:, :], ACT.Sqrt).then_inc(dev_ready, 1)
            for g in range(TILES // BLK):
                act.wait_ge(turned, g + 1)
                b, at = g // (QT // BLK), 1 + (g % (QT // BLK)) * BANK
                nc.scalar.activation(xnT[:, b, at:at + BANK], bank[g][:, :], ACT.Copy).then_inc(copied, 1)

        @block.tensor
        def _(pe):
            for i in range(TILES):
                pe.wait_ge(xn_ready, i + 1)
                j = i % BLK
                ins = nc.tensor.transpose(bank[i // BLK][:, j * P:(j + 1) * P], xn[:, i, :], ident[:, :])
                if j == BLK - 1:
                    ins.then_inc(turned, 1)





def attention(nc, name, is_a, hu, KS, V, O_all, QS, ident, window, xnT, wq_dram, bias_dram, QS4, hmask):
    heads = A_HEADS if is_a else B_HEADS
    dh = A_DH if is_a else B_DH
    its, S = heads // hu, QT * hu
    TC = sum(1 if qt < BLK else 2 for qt in range(QT)) * hu
    NSLOT, RING = 6, 8
    PROJ = SEQ // BANK if is_a else 0
    FIRST_MOVED = PROJ // 2 if is_a else 1
    uses = TC + PROJ * hu
    win_max = BIAS_W if is_a else P
    scale = -(A_DH ** -0.5)
    assert TC % NSLOT == 0 and uses % 2 == 0 and S % RING == 0

    def chunks(k):
        return range(1 if k % QT < BLK else 2)

    def blocks(k, c):
        return range(c * BLK, min(k % QT + 1, (c + 1) * BLK))

    def on_dve(k, c):
        return k % QT < BLK or c == 1

    def numbering(last):
        t, p, n = {}, {}, 0
        for k in range(S):
            for c in chunks(k):
                t[k, c], n = n, n + 1
            if k % QT == 1 and not (last and k // QT == hu - 1):
                for c in range(PROJ):
                    p[k // QT, c], n = n, n + 1
        return t, p

    chunk_no = {kc: i for i, kc in enumerate((k, c) for k in range(S) for c in chunks(k))}
    far_no = {j: i for i, j in enumerate(j for j in range(S) if P * (j % QT + 1) > win_max)}

    with Phase(nc, name) as ph:
        score = [ph.psum(f"score{i}", [P, 2 * BANK]) for i in range(2)]
        pt = [ph.psum(f"pt{i}", [P, BANK]) for i in range(2)]
        o_ps = [ph.psum(f"o{i}", [P, BANK]) for i in range(2)]
        prob = [ph.sb(f"prob{i}", [P, SEQ]) for i in range(2)]
        pts = [ph.sb(f"pts{i}", [P, BANK]) for i in range(NSLOT)]
        m_far, m_all = ph.sb("m_far", [P, RING]), ph.sb("m_all", [P, RING])
        scratch, pool_scratch = ph.sb("scratch", [P, 1]), ph.sb("pool_scratch", [P, 1])
        rowsum, rinv = ph.sb("rowsum", [P, RING]), ph.sb("rinv", [P, RING])
        qk_done, max_done, exp_done = ph.sem("qk_done"), ph.sem("max_done"), ph.sem("exp_done")
        far_done, inv_done = ph.sem("far_done"), ph.sem("inv_done")
        pt_done, slot_free, o_free = ph.sem("pt_done"), ph.sem("slot_free"), ph.sem("o_free")
        moved = [ph.sem(f"moved{i}") for i in range(2)]
        qs_ready, hi_done = ph.sem("qs_ready"), ph.sem("hi_done")
        placed, pool_placed = ph.sem("placed"), ph.sem("pool_placed")
        if is_a:
            wq = [ph.sb(f"wq{i}", [P, 2, A_DH]) for i in range(2)]
            bt = [ph.sb(f"bt{i}", [P, BIAS_W]) for i in range(2)]
            wq_ready = [ph.sem(f"wq_ready{i}") for i in range(2)]
            bt_ready = [ph.sem(f"bt_ready{i}") for i in range(2)]
        block = ph.block()

        def halves(it, n):
            return it * (uses // 2) + FIRST_MOVED + n // 2

        def loads(it, u):
            return (it * (hu // 2) + u // 2 + 1) * 16

        def run(eng, start, body):
            for b in range(BATCH):
                start(b)
                with eng.Fori(0, its - 1) as i:
                    body(b, i + b * its, i, False)
                body(b, b * its + its - 1, its - 1, True)

        @block.tensor
        def _(pe):
            pe.sem_inc(slot_free, NSLOT)
            if not is_a:
                for sem in moved:
                    pe.sem_inc(sem, FIRST_MOVED)

            def project(b, it, u, n0):
                pe.wait_ge(wq_ready[u % 2], loads(it, u))
                for c in range(PROJ):
                    if n0 is not None:
                        pe.wait_ge(moved[(n0[1] + c) % 2], n0[0] + (n0[1] + c) // 2)
                    bank = pt[c if n0 is None else (n0[1] + c) % 2]
                    nc.tensor.matmul(bank[:, :], wq[u % 2][:, :, :].rearrange("p a d -> p (a d)"),
                                     xnT[:, b, 1 + c * BANK:1 + (c + 1) * BANK],
                                     start=True, stop=True).then_inc(pt_done, 1)

            def scores(b, itl, j, ready):
                u, qt = j // QT, j % QT
                if qt == 0:
                    for sem, value in ready:
                        pe.wait_ge(sem, value)
                for c0 in range(0, P * (qt + 1), BANK):
                    w = max(min(BANK, P * (qt + 1) - c0), 2 * P)
                    at = b * SEQ + c0
                    parts = [k[:, at:at + w] for k in KS] if is_a else [KS[0][:, itl, at:at + w]]
                    for n, part in enumerate(parts):
                        ins = nc.tensor.matmul(score[j % 2][:, c0:c0 + w], QS[u % 2][:, qt * P:(qt + 1) * P],
                                               part, start=n == 0, stop=n == len(parts) - 1)
                ins.then_inc(qk_done, 1)

            def ready_after(it, u, p_no):
                if is_a:
                    return [(moved[p_no[u, c] % 2], halves(it, p_no[u, c]) + 1) for c in range(PROJ)]
                return [(qs_ready, it * hu + u + 2)]

            def start(b):
                if is_a:
                    project(b, b * its, 0, None if b == 0 else (b * its * uses // 2, 0))
                    ready = [(moved[c], b * its * uses // 2 + 1) for c in range(PROJ)]
                else:
                    ready = [(qs_ready, b * its * hu + 1)]
                scores(b, 0, 0, ready)
                scores(b, 0, 1, None)

            def body(b, it, itl, last):
                t_no, p_no = numbering(last)

                def output(k):
                    pe.wait_ge(o_free, it * S + k + 1)
                    for c in chunks(k):
                        n, i = t_no[k, c], chunk_no[k, c]
                        pe.wait_ge(moved[n % 2], halves(it, n) + 1)
                        for blk in blocks(k, c):
                            ins = nc.tensor.matmul(o_ps[k % 2][:, 0:P],
                                                   pts[i % NSLOT][:, (blk % BLK) * P:(blk % BLK + 1) * P],
                                                   V[:, b * QT + blk, :], start=blk == 0, stop=blk == k % QT)
                        ins.then_inc(slot_free, 1)

                for k in range(S):
                    pe.wait_ge(exp_done, it * S + k + 1)
                    for c in chunks(k):
                        n = t_no[k, c]
                        pe.wait_ge(moved[n % 2], halves(it, n))
                        for blk in blocks(k, c):
                            ins = nc.tensor.transpose(pt[n % 2][:, (blk % BLK) * P:(blk % BLK + 1) * P],
                                                      prob[k % 2][:, blk * P:(blk + 1) * P], ident[:, :])
                        ins.then_inc(pt_done, 1)
                    if (k // QT, 0) in p_no and k % QT == 1:
                        u = k // QT
                        project(b, it, u + 1, (halves(it, 0), p_no[u, 0]))
                    if k + 2 < S:
                        scores(b, itl, k + 2, ready_after(it, (k + 2) // QT - 1, p_no) if (k + 2) % QT == 0 else None)
                    elif not last:
                        scores(b, itl + 1, k + 2 - S, ready_after(it, hu - 1, p_no))
                    if k > 0:
                        output(k - 1)
                output(S - 1)

            run(pe, start, body)

        @block.vector
        def _(dve):
            dve.sem_inc(o_free, 2)

            def row_max(it, j, between):
                u, qt, r = j // QT, j % QT, j % RING
                nk = P * (qt + 1)
                win = min(nk, win_max)
                least = 3e38
                table = window
                if is_a:
                    table = bt[u % 2][:, BIAS_W - win:BIAS_W]
                if nk > win:
                    dve.wait_ge(qk_done, it * S + j + 1)
                    least = m_far[:, r:r + 1]
                    nc.vector.tensor_reduce(least, score[j % 2][:, 0:nk - win], AX.X, ALU.min).then_inc(far_done, 1)
                    dve.wait_ge(far_done, it * len(far_no) + far_no[j] + 1)
                else:
                    if is_a and qt == 0:
                        dve.wait_ge(bt_ready[u % 2], loads(it, u))
                    dve.wait_ge(qk_done, it * S + j + 1)
                between()
                near = score[j % 2][:, nk - win:nk]
                nc.vector.tensor_tensor_reduce(out=near, in0=near, in1=table, scale=1.0, scalar=least,
                                               op0=ALU.add, op1=ALU.min,
                                               accum_out=m_all[:, r:r + 1]).then_inc(max_done, 1)

            def place(n):
                if n is not None:
                    dve.wait_ge(placed, n)
                nc.vector.memset(scratch[:, :], 0.0).then_inc(placed, 1)

            def invert(it, k):
                r = k % RING
                dve.wait_ge(exp_done, it * S + k + 1)
                nc.vector.reciprocal(rinv[:, r:r + 1], rowsum[:, r:r + 1]).then_inc(inv_done, 1)

            def norm(b, it, itl, k):
                r = k % RING
                i = chunk_no[k, chunks(k)[-1]]
                dve.wait_ge(slot_free, it * TC + NSLOT + i + 1)
                dve.wait_ge(inv_done, it * S + k + 1)
                at = (itl * hu + k // QT) * dh
                src = o_ps[k % 2][:, 0:dh] if is_a else o_ps[k % 2][:, bass.ds(at, dh)]
                nc.vector.tensor_scalar(O_all[:, b * QT + k % QT, bass.ds(at, dh)], src, rinv[:, r:r + 1],
                                        None, ALU.mult).then_inc(o_free, 1)

            def low_parts(head, u, first):
                for c in range(PROJ):
                    dve.wait_ge(hi_done, head * PROJ + c + 1)
                    lo = QS[u % 2][A_DH:P, c * BANK:(c + 1) * BANK]
                    bank = (first + c) % 2
                    nc.vector.scalar_tensor_tensor(lo, pt[bank][A_DH:P, :], scale, lo.bitcast(F32),
                                                   ALU.mult, ALU.subtract).then_inc(moved[bank], 1)

            def start(b):
                if is_a:
                    low_parts(b * heads, 0, 0)
                row_max(b * its, 0, lambda: place(b * (its + 1) if b else None))

            def body(b, it, itl, last):
                t_no, p_no = numbering(last)
                for k in range(S):
                    def between():
                        if k > 0:
                            invert(it, k - 1)
                        else:
                            place(it + b + 1)

                    if k + 1 < S:
                        row_max(it, k + 1, between)
                    elif not last:
                        row_max(it + 1, 0, between)
                    else:
                        between()
                    if k > 1:
                        norm(b, it, itl, k - 2)
                    for c in chunks(k):
                        if on_dve(k, c):
                            n, i, w = t_no[k, c], chunk_no[k, c], P * len(blocks(k, c))
                            dve.wait_ge(pt_done, it * uses + PROJ + n + 1)
                            dve.wait_ge(slot_free, it * TC + i + 1)
                            nc.vector.tensor_copy(pts[i % NSLOT][:, 0:w], pt[n % 2][:, 0:w]).then_inc(moved[n % 2], 1)
                    if (k // QT, 0) in p_no and k % QT == 1:
                        u = k // QT
                        low_parts(it * hu + u + 1, u + 1, p_no[u, 0])
                invert(it, S - 1)
                norm(b, it, itl, S - 2)
                norm(b, it, itl, S - 1)

            run(dve, start, body)

        @block.scalar
        def _(act):
            def exp(it, j):
                r, nk = j % RING, P * (j % QT + 1)
                act.wait_ge(max_done, it * S + j + 1)
                nc.scalar.activation(prob[j % 2][:, 0:nk], score[j % 2][:, 0:nk], ACT.Exp, bias=m_all[:, r:r + 1],
                                     scale=-1.0, accum_out=rowsum[:, r:r + 1]).then_inc(exp_done, 1)

            def high_parts(u, first, use):
                for c in range(PROJ):
                    act.wait_ge(pt_done, use + c + 1)
                    nc.scalar.activation(QS[u % 2][:, c * BANK:(c + 1) * BANK], pt[(first + c) % 2][:, :],
                                         ACT.Copy, scale=scale).then_inc(hi_done, 1)

            def start(b):
                if is_a:
                    high_parts(0, 0, b * its * uses)
                exp(b * its, 0)

            def body(b, it, itl, last):
                t_no, p_no = numbering(last)
                for k in range(S):
                    if k + 1 < S:
                        exp(it, k + 1)
                    elif not last:
                        exp(it + 1, 0)
                    for c in chunks(k):
                        if not on_dve(k, c):
                            n, i, w = t_no[k, c], chunk_no[k, c], P * len(blocks(k, c))
                            act.wait_ge(pt_done, it * uses + PROJ + n + 1)
                            act.wait_ge(slot_free, it * TC + i + 1)
                            nc.scalar.activation(pts[i % NSLOT][:, 0:w], pt[n % 2][:, 0:w], ACT.Copy).then_inc(moved[n % 2], 1)
                    if (k // QT, 0) in p_no and k % QT == 1:
                        u = k // QT
                        high_parts(u + 1, p_no[u, 0], it * uses + PROJ + p_no[u, 0])

            run(act, start, body)

        if is_a:
            @block.sync
            def _(sp):
                def load(head, u):
                    sp.dma_start(wq[u % 2][:, :, :], bass.AP(tensor=wq_dram.tensor, offset=head * A_DH,
                                                            ap=[[A_HEADS * A_DH, P], [0, 2], [1, A_DH]])
                                 ).then_inc(wq_ready[u % 2], 16)
                    sp.dma_start(bt[u % 2][:, :], bias_dram[bass.ds(head * P, P), :]).then_inc(bt_ready[u % 2], 16)

                def start(b):
                    if b == 0:
                        load(0, 0)

                def body(b, it, itl, last):
                    for u in range(hu):
                        if last and u == hu - 1 and b == BATCH - 1:
                            continue
                        sp.wait_ge(max_done, it * S + u * QT + 1)
                        load(0 if last and u == hu - 1 else itl * hu + u + 1, u + 1)

                run(sp, start, body)
        else:
            @block.gpsimd
            def _(pool):
                def queries(b, itl, u, value, turn=None):
                    if turn is not None:
                        pool.wait_ge(pool_placed, turn)
                    if value is not None:
                        pool.wait_ge(qk_done, value)
                    nc.gpsimd.tensor_tensor(pool_scratch[:, :], hmask[:, 0:1], hmask[:, 0:1],
                                            ALU.mult).then_inc(pool_placed, 1)
                    nc.gpsimd.tensor_tensor(QS[u % 2][:, :], QS4[:, itl, b * SEQ:(b + 1) * SEQ].bitcast(F32),
                                            hmask[:, u % GRP:u % GRP + 1].to_broadcast([P, SEQ]),
                                            ALU.mult).then_inc(qs_ready, 1)

                def start(b):
                    queries(b, 0, 0, b * its * S if b else None, b * its * hu if b else None)

                def body(b, it, itl, last):
                    for u in range(hu):
                        if u + 1 < hu:
                            queries(b, itl, u + 1, (it * hu + u) * QT + 1, it * hu + u + 1)
                        elif not last:
                            queries(b, itl + 1, 0, (it * hu + u) * QT + 1, it * hu + u + 1)

                run(pool, start, body)


def project_out(nc, name, O_all, blocks, w_out, bias, X, ident):
    with Phase(nc, name) as ph:
        pt = [ph.psum(f"pt{i}", [P, BANK]) for i in range(4)]
        y_ps = [ph.psum(f"y{i}", [P, BANK]) for i in range(2)]
        oT = [ph.sb(f"oT{i}", [P, blocks, P]) for i in range(2)]
        turned, y_done, y_used = ph.sem("turned"), ph.sem("y_done"), ph.sem("y_used")
        moved_act, biased = ph.sem("moved_act"), ph.sem("biased")
        block = ph.block()
        per = (blocks + BLK - 1) // BLK

        def part(c):
            return range(c * BLK, min(blocks, (c + 1) * BLK))

        @block.tensor
        def _(pe):
            def turn(i):
                for c in range(per):
                    n = i * per + c
                    if n >= 4:
                        pe.wait_ge(moved_act, n - 3)
                    for j in part(c):
                        ins = nc.tensor.transpose(pt[n % 4][:, (j % BLK) * P:(j % BLK + 1) * P],
                                                  O_all[:, i, j * P:(j + 1) * P], ident[:, :])
                    ins.then_inc(turned, 1)

            turn(0)
            for i in range(TILES):
                if i + 1 < TILES:
                    turn(i + 1)
                pe.wait_ge(moved_act, (i + 1) * per)
                if i >= 2:
                    pe.wait_ge(y_used, i - 1)
                for j in range(blocks):
                    ins = nc.tensor.matmul(y_ps[i % 2][:, 0:P], oT[i % 2][:, j, :], w_out[:, j, :],
                                           start=j == 0, stop=j == blocks - 1)
                ins.then_inc(y_done, 1)

        @block.scalar
        def _(act):
            for i in range(TILES):
                if i >= 2:
                    act.wait_ge(y_done, i - 1)
                for c in range(per):
                    act.wait_ge(turned, i * per + c + 1)
                    w = P * len(part(c))
                    nc.scalar.activation(oT[i % 2][:, c * BLK:c * BLK + len(part(c)), :].rearrange("p j q -> p (j q)"),
                                         pt[(i * per + c) % 4][:, 0:w], ACT.Copy).then_inc(moved_act, 1)

        @block.vector
        def _(dve):
            nc.vector.tensor_tensor(X[:, :, :], X[:, :, :], bias[:, :].unsqueeze(1).to_broadcast([P, TILES, D]),
                                    ALU.add).then_inc(biased, 1)
            dve.wait_ge(biased, 1)
            for i in range(TILES):
                dve.wait_ge(y_done, i + 1)
                nc.vector.tensor_tensor(X[:, i, :], X[:, i, :], y_ps[i % 2][:, 0:D], ALU.add).then_inc(y_used, 1)


def prepare_a(nc, xnT, wkv, KH, KL, Vd):
    with Phase(nc, "prep_a") as ph:
        kp = [ph.psum(f"k{i}", [P, BANK]) for i in range(4)]
        vp = [ph.psum(f"v{i}", [P, BANK]) for i in range(4)]
        k_done, v_done, high = ph.sem("k_done"), ph.sem("v_done"), ph.sem("high")
        block = ph.block()

        @block.tensor
        def _(pe):
            for g in range(4):
                b, at = g // 2, 1 + (g % 2) * BANK
                nc.tensor.matmul(kp[g][:, :], wkv[:, 0, :], xnT[:, b, at:at + BANK],
                                 start=True, stop=True).then_inc(k_done, 1)
            for i in range(TILES):
                at = 1 + (i % QT) * P
                ins = nc.tensor.matmul(vp[i // BLK][:, (i % BLK) * P:(i % BLK + 1) * P],
                                       xnT[:, i // QT, at:at + P], wkv[:, 1, :], start=True, stop=True)
                if i % BLK == BLK - 1:
                    ins.then_inc(v_done, 1)

        @block.scalar
        def _(act):
            for g in range(4):
                act.wait_ge(k_done, g + 1)
                nc.scalar.activation(KH[:, g * BANK:(g + 1) * BANK], kp[g][:, :], ACT.Copy).then_inc(high, 1)
            for g in range(4):
                act.wait_ge(v_done, g + 1)
                nc.scalar.activation(Vd[:, g * BLK:(g + 1) * BLK, :].rearrange("p t d -> p (t d)"), vp[g][:, :], ACT.Copy)

        @block.vector
        def _(dve):
            for g in range(4):
                dve.wait_ge(high, g + 1)
                nc.vector.tensor_tensor(KL[:, g * BANK:(g + 1) * BANK], kp[g][:, :],
                                        KH[:, g * BANK:(g + 1) * BANK].bitcast(F32), ALU.subtract)


def route(nc, name, xnT, router, consts, slot, gate):
    upper, ones_bf, prio, ebase, spare = consts
    with Phase(nc, name) as ph:
        logit, count, total = (ph.psum(n, [P, BANK // E, E])[:, 0:TILES, :] for n in ("logit", "count", "total"))
        a, ex, mask = ph.sb("a", [P, TILES, E]), ph.sb("ex", [P, TILES, E]), ph.sb("mask", [P, TILES, E])
        mask_bf = ph.sb("mask_bf", [P, TILES, E], BF16)
        tot, run, one = ph.sb("tot", [P, TILES, E]), ph.sb("run", [P, TILES, E]), ph.sb("one", [P, TILES])
        m1, m2, pos = ph.sb("m1", [P, TILES]), ph.sb("m2", [P, TILES]), ph.sb("pos", [P, TILES])
        keep, row = ph.sb("keep", [P, TILES]), ph.sb("row", [P, TILES])
        chain, logits, shifted, exped = ph.sem("chain"), ph.sem("logits"), ph.sem("shifted"), ph.sem("exped")
        masked, counted = ph.sem("masked"), ph.sem("counted")
        block = ph.block()

        def wide(x):
            return x[:, :].unsqueeze(2).to_broadcast([P, TILES, E])

        @block.tensor
        def _(pe):
            for i in range(TILES):
                at = 1 + (i % QT) * P
                ins = nc.tensor.matmul(logit[:, i, :], xnT[:, i // QT, at:at + P], router[:, :], start=True, stop=True)
            ins.then_inc(logits, 1)
            pe.wait_ge(masked, 1)
            flat = mask_bf[:, :, :].rearrange("p t e -> p (t e)")
            nc.tensor.matmul(count[:, :, :].rearrange("p t e -> p (t e)"), upper[:, :], flat, start=True, stop=True)
            nc.tensor.matmul(total[:, :, :].rearrange("p t e -> p (t e)"), ones_bf[:, :], flat,
                             start=True, stop=True).then_inc(counted, 1)

        @block.scalar
        def _(act):
            act.wait_ge(shifted, 1)
            nc.scalar.activation(ex[:, :, :], a[:, :, :], ACT.Exp).then_inc(exped, 1)

        @block.vector
        def _(dve):
            link = Chain(dve, chain)
            nc.vector.memset(one[:, :], 1.0)
            dve.wait_ge(logits, 1)
            link(nc.vector.tensor_reduce(m1[:, :], logit[:, :, :], AX.X, ALU.max))
            nc.vector.tensor_tensor(a[:, :, :], logit[:, :, :], wide(m1), ALU.subtract).then_inc(shifted, 1)
            dve.wait_ge(exped, 1)
            link(nc.vector.tensor_reduce(m2[:, :], ex[:, :, :], AX.X, ALU.add))
            link(nc.vector.tensor_reduce(m1[:, :], ex[:, :, :], AX.X, ALU.max))
            link(nc.vector.reciprocal(keep[:, :], m2[:, :]))
            link(nc.vector.tensor_tensor(gate[:, :], m1[:, :], keep[:, :], ALU.mult))
            link(nc.vector.tensor_tensor(a[:, :, :], ex[:, :, :], wide(m1), ALU.is_equal))
            link(nc.vector.tensor_tensor(a[:, :, :], a[:, :, :], prio[:, :, :], ALU.mult))
            link(nc.vector.tensor_reduce(m2[:, :], a[:, :, :], AX.X, ALU.max))
            link(nc.vector.tensor_tensor(mask[:, :, :], a[:, :, :], wide(m2), ALU.is_equal))
            nc.vector.tensor_copy(mask_bf[:, :, :], mask[:, :, :]).then_inc(masked, 1)
            dve.wait_ge(counted, 1)
            link(nc.vector.tensor_copy(tot[:, :, :], total[:, :, :]))
            for e in range(E):
                ins = nc.vector.tensor_tensor_scan(run[:, :, e], one[:, :], tot[:, :, e], 0.0, ALU.mult, ALU.add)
            link(ins)
            link(nc.vector.tensor_tensor(run[:, :, :], run[:, :, :], tot[:, :, :], ALU.subtract))
            link(nc.vector.tensor_tensor(run[:, :, :], run[:, :, :], count[:, :, :], ALU.add))
            link(nc.vector.tensor_tensor(run[:, :, :], run[:, :, :], mask[:, :, :], ALU.mult))
            link(nc.vector.tensor_reduce(pos[:, :], run[:, :, :], AX.X, ALU.add))
            link(nc.vector.tensor_tensor(a[:, :, :], mask[:, :, :], ebase[:, :, :], ALU.mult))
            link(nc.vector.tensor_reduce(row[:, :], a[:, :, :], AX.X, ALU.add))
            link(nc.vector.tensor_scalar(keep[:, :], pos[:, :], float(CAP), None, ALU.is_le))
            link(nc.vector.tensor_tensor(row[:, :], row[:, :], pos[:, :], ALU.add))
            link(nc.vector.tensor_tensor(row[:, :], row[:, :], spare[:, :], ALU.subtract))
            link(nc.vector.tensor_tensor(row[:, :], row[:, :], keep[:, :], ALU.mult))
            link(nc.vector.tensor_tensor(row[:, :], row[:, :], spare[:, :], ALU.add))
            nc.vector.tensor_scalar(slot[:, :], row[:, :], -1.0, None, ALU.add)


def experts(nc, name, xn, X, slot, gate, b1T, b2_dram, w1_dram, w2_dram, xe_dram, ye_dram, ident, ones):
    with Phase(nc, name) as ph:
        NW = 2
        w1 = [ph.sb(f"w1_{i}", [P, F]) for i in range(NW)]
        w2 = [ph.sb(f"w2_{i}", [P, FB, D]) for i in range(NW)]
        b2 = [ph.sb(f"b2_{i}", [1, D]) for i in range(NW)]
        xe = [ph.sb(f"xe{i}", [P, 2, D]) for i in range(NW)]
        xeT = [ph.sb(f"xeT{i}", [P, CAP]) for i in range(NW)]
        hT = [ph.sb(f"hT{i}", [P, FB, CAP]) for i in range(NW)]
        ye = [ph.sb(f"ye{i}", [P, 2, D]) for i in range(NW)]
        back = ph.sb("back", [P, TILES, D])
        t_ps = [ph.psum(f"t{i}", [P, BANK])[:, 0:CAP] for i in range(2)]
        h_ps = [ph.psum(f"h{i}", [P, 2, CAP]) for i in range(4)]
        y_ps = [ph.psum(f"y{i}", [P, BLK, D])[:, 0:2, :] for i in range(2)]
        sent, w_ready = ph.sem("sent"), [ph.sem(f"w_ready{i}") for i in range(NW)]
        xe_ready = [ph.sem(f"xe_ready{i}") for i in range(NW)]
        turned, xeT_ready, h_done = ph.sem("turned"), ph.sem("xeT_ready"), ph.sem("h_done")
        relu_act, relu_dve, y_done, ye_ready = ph.sem("relu_act"), ph.sem("relu_dve"), ph.sem("y_done"), ph.sem("ye_ready")
        stored = [ph.sem(f"stored{i}") for i in range(NW)]
        fetched = ph.sem("fetched")
        block = ph.block()
        ITS = E // NW

        @block.gpsimd
        def _(pool):
            for i in range(TILES):
                pool.indirect_dma_start(out=xe_dram[:, :], out_offset=bass.IndirectOffsetOnAxis(ap=slot[:, i:i + 1], axis=0),
                                        in_=xn[:, i, :], in_offset=None).then_inc(sent, 16)
            for i in range(NW):
                pool.wait_ge(stored[i], 16 * (ITS + 1))
            for i in range(TILES):
                pool.indirect_dma_start(out=back[:, i, :], out_offset=None, in_=ye_dram[:, :],
                                        in_offset=bass.IndirectOffsetOnAxis(ap=slot[:, i:i + 1], axis=0)).then_inc(fetched, 16)

        @block.sync
        def _(sp):
            def weights(e, i):
                sp.dma_start(w1[i][:, :], bass.AP(tensor=w1_dram.tensor, offset=e * (D * F), ap=[[F, P], [1, F]])).then_inc(w_ready[i], 16)
                sp.dma_start(w2[i][:, :, :], bass.AP(tensor=w2_dram.tensor, offset=e * (F * D),
                                                     ap=[[D, P], [P * D, FB], [1, D]])).then_inc(w_ready[i], 16)
                sp.dma_start(b2[i][:, :], bass.AP(tensor=b2_dram.tensor, offset=e * D, ap=[[D, 1], [1, D]])).then_inc(w_ready[i], 16)

            def rows(e, i):
                sp.dma_start(xe[i][:, :, :], bass.AP(tensor=xe_dram, offset=e * (CAP * D),
                                                     ap=[[D, P], [P * D, 2], [1, D]])).then_inc(xe_ready[i], 16)

            for i in range(NW):
                weights(i, i)
            sp.wait_ge(sent, 16 * TILES)
            for i in range(NW):
                rows(i, i)

            def body(it, last):
                for i in range(NW):
                    if not last:
                        sp.wait_ge(y_done, it * NW + i + 1)
                        weights((it + 1) * NW + i, i)
                        rows((it + 1) * NW + i, i)
                    sp.wait_ge(ye_ready, it * NW + i + 2)
                    sp.dma_start(bass.AP(tensor=ye_dram, offset=(it * NW + i) * (CAP * D),
                                         ap=[[D, P], [P * D, 2], [1, D]]), ye[i][:, :, :]).then_inc(stored[i], 16)

            with sp.Fori(0, ITS - 1) as it:
                body(it, False)
            body(ITS - 1, True)

        @block.tensor
        def _(pe):
            for sem in (xeT_ready, relu_act, relu_dve, ye_ready):
                pe.sem_inc(sem, 1)
            for sem in stored:
                pe.sem_inc(sem, 16)

            def body(it):
                for i in range(NW):
                    n = it * NW + i
                    pe.wait_ge(xe_ready[i], (it + 1) * 16)
                    pe.wait_ge(xeT_ready, n + 1)
                    for c in range(2):
                        ins = nc.tensor.transpose(t_ps[i][:, c * P:(c + 1) * P], xe[i][:, c, :], ident[:, :])
                    ins.then_inc(turned, 1)
                    pe.wait_ge(xeT_ready, n + 2)
                    pe.wait_ge(w_ready[i], (it + 1) * 48)
                    pe.wait_ge(relu_act, n + 1)
                    pe.wait_ge(relu_dve, n + 1)
                    for f in range(FB):
                        ins = nc.tensor.matmul(h_ps[2 * (i % 2) + f // 2][:, f % 2, :], w1[i][:, f * P:(f + 1) * P], xeT[i][:, :],
                                               start=True, stop=True)
                        if f % 2:
                            ins.then_inc(h_done, 1)
                    pe.wait_ge(relu_act, n + 2)
                    pe.wait_ge(relu_dve, n + 2)
                    pe.wait_ge(ye_ready, n + 1)
                    for c in range(2):
                        for f in range(FB):
                            nc.tensor.matmul(y_ps[i % 2][:, c, :], hT[i][:, f, c * P:(c + 1) * P], w2[i][:, f, :],
                                             start=f == 0, stop=False)
                        ins = nc.tensor.matmul(y_ps[i % 2][:, c, :], ones[0:1, :], b2[i][0:1, :], start=False, stop=True)
                    ins.then_inc(y_done, 1)

            with pe.Fori(0, ITS) as it:
                body(it)

        @block.scalar
        def _(act):
            def body(it):
                for i in range(NW):
                    n = it * NW + i
                    act.wait_ge(turned, n + 1)
                    nc.scalar.activation(xeT[i][:, :], t_ps[i][:, :], ACT.Copy).then_inc(xeT_ready, 1)
                    act.wait_ge(h_done, 2 * n + 1)
                    for f in range(2):
                        ins = nc.scalar.activation(hT[i][:, f, :], h_ps[2 * (i % 2)][:, f, :], ACT.Relu,
                                                   bias=b1T[:, f, bass.ds(n, 1)])
                    ins.then_inc(relu_act, 1)

            with act.Fori(0, ITS) as it:
                body(it)

        @block.vector
        def _(dve):
            def body(it):
                for i in range(NW):
                    n = it * NW + i
                    dve.wait_ge(h_done, 2 * n + 2)
                    for f in range(2, FB):
                        ins = nc.vector.tensor_scalar(hT[i][:, f, :], h_ps[2 * (i % 2) + 1][:, f % 2, :],
                                                      b1T[:, f, bass.ds(n, 1)], 0.0, ALU.add, ALU.max)
                    ins.then_inc(relu_dve, 1)
                    dve.wait_ge(y_done, n + 1)
                    dve.wait_ge(stored[i], (it + 1) * 16)
                    nc.vector.tensor_copy(ye[i][:, :, :], y_ps[i % 2][:, :, :]).then_inc(ye_ready, 1)

            with dve.Fori(0, ITS) as it:
                body(it)
            for i in range(TILES):
                dve.wait_ge(fetched, 16 * TILES)
                nc.vector.scalar_tensor_tensor(X[:, i, :], back[:, i, :], gate[:, i:i + 1], X[:, i, :], ALU.mult, ALU.add)


def geometry(nc, xnT, w_geo, sel, row_decay, scale_row, kv_gate, gate, ident):
    H = B_HEADS
    with Phase(nc, "geo") as ph:
        G = ph.sb("G", [P, TILES, 4, H, 4])
        L, Ls = ph.sb("L", [P, TILES, 2, H, 9]), ph.sb("Ls", [P, TILES, 2, H, 9])
        T = ph.sb("T", [P, TILES, 2 * H])
        nrm, inv = ph.sb("nrm", [P, TILES, 2 * H]), ph.sb("inv", [P, TILES, 2 * H])
        prod = [ph.sb(f"prod{w}", [P, TILES, PAIRS, H]) for w in range(2)]
        g_done, g_moved, chain, lines = ph.sem("g_done"), ph.sem("g_moved"), ph.sem("chain"), ph.sem("lines")
        made = [ph.sem(f"made{w}") for w in range(2)]
        turned, used = ph.sem("turned"), ph.sem("used")
        M = [ph.sb(f"M{i}", [ROWS, SEQ + 1]) for i in range(2)]
        RM = ph.sb("RM", [ROWS, 3, TOK])
        scanned, scored, nz, ez = ph.sem("scanned"), ph.sem("scored"), ph.sem("nz"), ph.sem("ez")
        bank = [ph.psum(f"bank{i}", [P, BANK]) for i in range(7)]
        s_ps = ph.psum("s", [P, TILES, H])
        z, e1 = ph.sb("z", [P, TILES, H]), ph.sb("e1", [P, TILES, H])
        decay_b = row_decay[0:ROWS, 0:1].to_broadcast([ROWS, SEQ])
        block = ph.block()
        order = [(b, g, w, c) for b in range(BATCH) for g in range(3) for w in range(2) for c in range(2)]

        @block.tensor
        def _(pe):
            for i in range(TILES):
                at, b, o = (i % QT) * P, i // QT, (i % 2) * 4 * H * 4
                if i % 2 == 0 and i // 2 >= 7:
                    pe.wait_ge(g_moved, i // 2 - 6)
                out = bank[(i // 2) % 7]
                nc.tensor.matmul(out[:, o:o + 64], xnT[:, b, at:at + P], w_geo[:, 0:64], start=True, stop=True)
                ins = nc.tensor.matmul(out[:, o + 64:o + 256], xnT[:, b, 1 + at:1 + at + P], w_geo[:, 64:256], start=True, stop=True)
                if i % 2:
                    ins.then_inc(g_done, 1)
            for n, (b, g, w, c) in enumerate(order):
                if (b, g, c) == (0, 0, 0):
                    pe.wait_ge(made[w], 1)
                if n < 7:
                    pe.wait_ge(g_moved, 8)
                else:
                    pe.wait_ge(used, n - 6)
                for j in range(BLK):
                    ins = nc.tensor.transpose(bank[n % 7][0:ROWS, j * P:(j + 1) * P],
                                              prod[w][:, b * QT + c * BLK + j, 7 * g:7 * g + 7, :].rearrange("p a h -> p (a h)"),
                                              ident[:, :])
                ins.then_inc(turned, 1)
            pe.wait_ge(used, len(order))
            for i in range(TILES):
                for g in range(3):
                    ins = nc.tensor.matmul(s_ps[:, i, :], RM[:, g, i * P:(i + 1) * P], sel[0:ROWS, g, :],
                                           start=g == 0, stop=g == 2)
            ins.then_inc(scored, 1)

        @block.scalar
        def _(act):
            for i in range(TILES // 2):
                act.wait_ge(g_done, i + 1)
                nc.scalar.activation(G[:, 2 * i:2 * i + 2, :, :, :].rearrange("p t a h c -> p (t a h c)"), bank[i % 7][:, :],
                                     ACT.Copy).then_inc(g_moved, 1)
            act.wait_ge(nz, 1)
            nc.scalar.activation(e1[:, :, :], z[:, :, :], ACT.Exp, scale=-1.0).then_inc(ez, 1)

        @block.vector
        def _(dve):
            link = Chain(dve, chain)
            dve.wait_ge(g_moved, TILES // 2)

            def pt(a, c):
                return G[:, :, 2 * a:2 * a + 2, :, c].rearrange("p t w h -> p t (w h)")

            def line(src, c):
                return src[:, :, :, :, c].rearrange("p t w h -> p t (w h)")

            for c, (i, j) in enumerate(((0, 1), (0, 2), (0, 3), (2, 3), (1, 3), (1, 2))):
                link(nc.vector.tensor_tensor(T[:, :, :], pt(0, j), pt(1, i), ALU.mult))
                link(nc.vector.tensor_tensor(line(L, c), pt(0, i), pt(1, j), ALU.mult))
                link(nc.vector.tensor_tensor(line(L, c), line(L, c), T[:, :, :], ALU.subtract))
            link(nc.vector.tensor_copy(L[:, :, :, :, 6:9].rearrange("p t w h c -> p (t w h) c"),
                                       L[:, :, :, :, 0:3].rearrange("p t w h c -> p (t w h) c")))
            flat = [x[:, :, :, :, :].rearrange("p t w h c -> p (t w h) c") for x in (L, Ls)]
            link(nc.vector.tensor_tensor(flat[1], flat[0], flat[0], ALU.mult))
            nflat, iflat = (x[:, :, :].rearrange("p t w -> p (t w)") for x in (nrm, inv))
            link(nc.vector.tensor_reduce(nflat, flat[1][:, :, 0:6], AX.X, ALU.add))
            link(nc.vector.tensor_scalar(nflat, nflat, 1e-24, None, ALU.max))
            link(nc.vector.reciprocal(iflat, nflat))
            link(nc.vector.tensor_tensor(flat[1], flat[0], iflat.unsqueeze(2).to_broadcast([P, TILES * 2 * H, 9]), ALU.mult))
            for w in range(2):
                o = 3 * w
                n = 0
                for a in range(6):
                    k = 6 - a
                    ins = nc.vector.tensor_tensor(
                        prod[w][:, :, n:n + k, :].rearrange("p t a h -> p t h a"),
                        L[:, :, w, :, o + a:o + a + 1].to_broadcast([P, TILES, H, k]),
                        Ls[:, :, w, :, o + a:o + 6], ALU.mult)
                    n += k
                ins.then_inc(made[w], 1)
            for i in range(2):
                link(nc.vector.memset(M[i][:, 0:1], 0.0))
            for b in range(BATCH):
                for g in range(3):
                    n = (b * 3 + g) * 4
                    m = M[g % 2]
                    for c in range(2):
                        dve.wait_ge(turned, n + c + 1)
                        nc.vector.tensor_tensor_scan(m[:, 1 + c * BANK:1 + (c + 1) * BANK], decay_b[:, 0:BANK],
                                                     bank[(n + c) % 7][0:ROWS, :],
                                                     0.0 if c == 0 else m[:, c * BANK:c * BANK + 1],
                                                     ALU.mult, ALU.add).then_inc(used, 1)
                        dve.wait_ge(used, n + c + 1)
                    for c in range(2):
                        dve.wait_ge(turned, n + c + 3)
                        ins = nc.vector.scalar_tensor_tensor(RM[:, g, b * SEQ + c * BANK:b * SEQ + (c + 1) * BANK],
                                                             bank[(n + 2 + c) % 7][0:ROWS, :], row_decay[0:ROWS, 0:1],
                                                             m[:, c * BANK:(c + 1) * BANK], ALU.mult, ALU.mult)
                        ins.then_inc(used, 1)
                        dve.wait_ge(used, n + c + 3)
            dve.wait_ge(scored, 1)
            nc.vector.tensor_tensor(z[:, :, :], s_ps[:, :, :], scale_row[:, :].unsqueeze(1).to_broadcast([P, TILES, H]),
                                    ALU.mult).then_inc(nz, 1)
            dve.wait_ge(ez, 1)
            link(nc.vector.tensor_scalar(e1[:, :, :], e1[:, :, :], 1.0, None, ALU.add))
            link(nc.vector.reciprocal(z[:, :, :], e1[:, :, :]))
            nc.vector.tensor_scalar(gate[:, :, :], z[:, :, :], kv_gate[:, 0:1], None, ALU.mult)


def prepare_b(nc, xnT, w_kv, kv_bias, w_q, q_bias, gate, QS4, KS4, Vb, hi_sign, lo_q, lo_k, ident):
    H = B_HEADS
    NG = H // GRP
    with Phase(nc, "prep_b") as ph:
        kv = ph.sb("kv", [P, TILES, 4, H, B_DH])
        rep = [ph.sb(f"rep{i}", [P, NG, GRP, REP, B_DH]) for i in range(2)]
        q = [ph.sb(f"q{i}", [P, BANK]) for i in range(2)]
        kv_ps = [ph.psum(f"kvp{i}", [P, BANK]) for i in range(2)]
        k_ps = [ph.psum(f"kp{i}", [P, BANK]) for i in range(2)]
        q_ps = [ph.psum(f"qp{i}", [P, BANK]) for i in range(2)]
        kv_done, kv_read, chain, rep_done = ph.sem("kv_done"), ph.sem("kv_read"), ph.sem("chain"), ph.sem("rep_done")
        k_done, k_high, k_free = ph.sem("k_done"), ph.sem("k_high"), ph.sem("k_free")
        q_done, q_copied, q_high, q_low = ph.sem("q_done"), ph.sem("q_copied"), ph.sem("q_high"), ph.sem("q_low")
        block = ph.block()
        QN = NG * TOK // BANK

        @block.tensor
        def _(pe):
            def keys(i):
                pe.wait_ge(rep_done, i + 1)
                if i >= 2:
                    pe.wait_ge(k_free, i - 1)
                for g in range(NG):
                    ins = nc.tensor.transpose(k_ps[i % 2][:, g * P:(g + 1) * P],
                                              rep[i % 2][:, g, :, :, :].rearrange("p a r d -> p (a r d)"), ident[:, :])
                ins.then_inc(k_done, 1)

            for i in range(TILES):
                at, b = 1 + (i % QT) * P, i // QT
                if i >= 2:
                    pe.wait_ge(kv_read, i - 1)
                nc.tensor.matmul(kv_ps[i % 2][:, :], xnT[:, b, at:at + P], w_kv[:, :], start=True, stop=True).then_inc(kv_done, 1)
                g, t = i // 4, i % 4
                if i >= 2:
                    pe.wait_ge(q_copied, i - 1)
                nc.tensor.matmul(q_ps[i % 2][:, :], w_q[:, g, :], xnT[:, t // 2, 1 + (t % 2) * BANK:1 + (t % 2 + 1) * BANK],
                                 start=True, stop=True).then_inc(q_done, 1)
                if i:
                    keys(i - 1)
            keys(TILES - 1)

        @block.scalar
        def _(act):
            for i in range(TILES):
                act.wait_ge(q_copied, i + 1)
                g, t = i // 4, i % 4
                nc.scalar.activation(QS4[:, g, t * BANK:(t + 1) * BANK], q[i % 2][:, :], ACT.Copy, scale=hi_sign[:, 0:1]).then_inc(q_high, 1)
                act.wait_ge(k_done, i + 1)
                nc.scalar.activation(KS4[:, :, i * P:(i + 1) * P], k_ps[i % 2][:, :].rearrange("p (g t) -> p g t", g=NG),
                                     ACT.Copy, scale=hi_sign[:, 1:2]).then_inc(k_high, 1)

        @block.vector
        def _(dve):
            link = Chain(dve, chain)

            def low(i):
                g, t = i // 4, i % 4
                dve.wait_ge(q_high, i + 1)
                dst = QS4[:, g, t * BANK:(t + 1) * BANK]
                nc.vector.scalar_tensor_tensor(dst, q[i % 2][:, :], lo_q, dst.bitcast(F32), ALU.mult, ALU.add).then_inc(q_low, 1)
                dve.wait_ge(k_high, i + 1)
                dst = KS4[:, :, i * P:(i + 1) * P]
                nc.vector.scalar_tensor_tensor(dst, k_ps[i % 2][:, :].rearrange("p (g t) -> p g t", g=NG), lo_k,
                                               dst.bitcast(F32), ALU.mult, ALU.add).then_inc(k_free, 1)

            for i in range(TILES):
                dve.wait_ge(kv_done, i + 1)
                link(nc.vector.tensor_tensor(kv[:, i, :, :, :].rearrange("p a h d -> p (a h d)"), kv_ps[i % 2][:, :],
                                             kv_bias[:, :], ALU.add))
                dve.sem_inc(kv_read, 1)
                for a in range(2):
                    geo = kv[:, i, 2 + a, :, :]
                    link(nc.vector.tensor_tensor(geo, geo, gate[:, i, :].unsqueeze(2).to_broadcast([P, H, B_DH]), ALU.mult))
                nc.vector.tensor_tensor(Vb[:, i, :].rearrange("p (h d) -> p h d", h=H), kv[:, i, 1, :, :], kv[:, i, 3, :, :], ALU.add)
                link(nc.vector.tensor_tensor(kv[:, i, 0, :, :], kv[:, i, 0, :, :], kv[:, i, 2, :, :], ALU.add))
                if i >= 2:
                    dve.wait_ge(k_done, i - 1)
                nc.vector.tensor_copy(rep[i % 2][:, :, :, :, :].rearrange("p g a r d -> p (g a) r d"),
                                      kv[:, i, 0, :, :].unsqueeze(2).to_broadcast([P, H, REP, B_DH])).then_inc(rep_done, 1)
                dve.wait_ge(q_done, i + 1)
                if i >= 2:
                    dve.wait_ge(q_low, i - 1)
                nc.vector.tensor_scalar(q[i % 2][:, :], q_ps[i % 2][:, :], q_bias[:, i // 4:i // 4 + 1], -(B_DH ** -0.5),
                                        ALU.add, ALU.mult).then_inc(q_copied, 1)
                if i:
                    low(i - 1)
            low(TILES - 1)


COLS, at = {}, 0
for key, width in (("ident", P), ("upper", P), ("ones", P), ("window", P), ("prio", TILES * E), ("ebase", TILES * E),
                   ("spare", TILES), ("sel", 3 * B_HEADS), ("hmask", GRP), ("sign", 2), ("low", 2), ("bucket", BIAS_M)):
    COLS[key] = (at, at + width)
    at += width
TABLE_W = at


def tables():
    t = np.zeros((P, TABLE_W), np.float32)

    def put(key, a):
        lo, hi = COLS[key]
        t[:a.shape[0], lo:hi] = a

    r = np.arange(P)
    put("ident", np.eye(P))
    put("upper", r[:, None] <= r[None, :])
    put("ones", np.ones((P, P)))
    put("window", np.where(r[None, :] > r[:, None], MASKED, 0.0))
    put("prio", np.tile(E - np.arange(E), (P, TILES)))
    put("ebase", np.tile(CAP * np.arange(E), (P, TILES)))
    put("spare", SLOTS + 1 + P * np.arange(TILES)[None, :] + r[:, None])
    pairs = [(a, b) for a in range(6) for b in range(a, 6)]
    sign = [1, -1, 1, 1, -1, 1]
    sel = np.zeros((ROWS, 3, B_HEADS))
    for n, (a, b) in enumerate(pairs):
        for h in range(B_HEADS):
            sel[(n % 7) * B_HEADS + h, n // 7, h] = sign[a] * sign[b] * (1 if a == b else 2)
    put("sel", sel.reshape(ROWS, -1))
    copy = (r // B_DH) % REP
    put("hmask", (r[:, None] // (P // GRP)) == np.arange(GRP)[None, :])
    low = np.stack([copy % 2, copy // 2], 1)
    put("sign", 1.0 - 2.0 * low)
    put("low", low)
    bucket = np.zeros((BUCKETS + 1, BIAS_M), np.float32)
    for m in range(BIAS_M):
        n = 2 * P - 1 - m
        if n < 0:
            bucket[BUCKETS, m] = MASKED
            continue
        half = BUCKETS // 2
        which = n
        if n >= half:
            which = min(half + int(np.log(np.float32(n) / half) / np.log(MAX_DIST / half) * (BUCKETS - half)), BUCKETS - 1)
        bucket[which, m] -= A_DH ** 0.5
        bucket[BUCKETS - 1, m] += A_DH ** 0.5
    put("bucket", bucket)
    return t


def build(nc, t, out):
    ctx = ExitStack()
    with ctx:
        def sb(name, shape, dt=F32):
            return ctx.enter_context(nc.sbuf_tensor(name, shape, dt))

        def dram(name, shape):
            return nc.dram_tensor(name, shape, F32, kind="Internal")

        X, xn, xnT = sb("X", [P, TILES, D]), sb("xn", [P, TILES, D]), sb("xnT", [P, BATCH, SEQ + 1])
        tab = sb("tab", [P, TABLE_W])
        col = {k: tab[:, lo:hi] for k, (lo, hi) in COLS.items()}
        ident = col["ident"]
        upper_bf, ones_bf = sb("upper_bf", [P, P], BF16), sb("ones_bf", [P, P], BF16)
        wkv = sb("wkv", [P, 2, 2, A_DH])
        woa, bouta = sb("woa", [P, A_HEADS * A_DH // P, D]), sb("bouta", [P, D])
        router, b1T = sb("router", [P, E]), sb("b1T", [P, FB, E])
        w_geo, qkvw, geow = sb("w_geo", [P, 4, 4 * B_HEADS]), sb("qkvw", [P, 3 * D]), sb("geow", [P, 2 * D])
        w_kv, w_q = sb("w_kv", [P, BANK]), sb("w_q", [P, B_HEADS // GRP, P])
        kv_bias, q_bias = sb("kv_bias", [P, BANK]), sb("q_bias", [P, B_HEADS // GRP])
        wob, boutb = sb("wob", [P, 1, D]), sb("boutb", [P, D])
        kv_gate, scale_row, decay = sb("kv_gate", [P, 1]), sb("scale_row", [P, B_HEADS]), sb("decay", [P, 1])
        slot, gate = sb("slot", [P, TILES], I32), sb("gate", [P, TILES])
        bias_dram = dram("bias_by_query_and_key", [A_HEADS * P, BIAS_W])
        by_dist_dram, xe_dram, ye_dram = dram("bias_by_distance", [B_HEADS, BIAS_M]), dram("to_experts", [SLOTS + TOK, D]), dram("from_experts", [SLOTS + TOK, D])

        def row(a, n, offset=0):
            return bass.AP(tensor=a.tensor, offset=offset, ap=[[0, P], [1, n]])

        with Phase(nc, "setup") as ph:
            rel = ph.sb("rel", [BUCKETS + 1, A_HEADS])
            g_sb = ph.sb("g_sb", [A_HEADS, BIAS_M])
            zero = ph.sb("zero", [P, TILES, D])
            g_ps = ph.psum("g", [P, BANK])
            loaded, one_row, g_done, g_ready, zeroed = (ph.sem(n) for n in ("loaded", "one_row", "g_done", "g_ready", "zeroed"))
            g_stored, decays, zfill, late = ph.sem("g_stored"), ph.sem("decays"), ph.sem("zfill"), ph.sem("late")
            dec_in, dec_e = ph.sb("dec_in", [P, 1]), ph.sb("dec_e", [P, 1])
            block = ph.block()
            LATE = 1 + 12 + 4

            @block.sync
            def _(sp):
                sp.dma_start(X[:, :, :], t["x"].rearrange("b (t p) d -> p (b t) d", p=P)).then_inc(late, 16)
                sp.dma_start(tab[:, :], t["table"]).then_inc(loaded, 16)
                sp.dma_start(rel[0:BUCKETS, :], t["rel_emb"]).then_inc(loaded, 16)
                for dst, src in (
                    [(wkv[:, 0, :, :], bass.AP(tensor=t["Wkv"].tensor, offset=0, ap=[[2 * A_DH, P], [0, 2], [1, A_DH]])),
                     (wkv[:, 1, :, :], bass.AP(tensor=t["Wkv"].tensor, offset=A_DH, ap=[[2 * A_DH, P], [0, 2], [1, A_DH]])),
                     (woa[:, :, :], t["Wout"].rearrange("(j p) d -> p j d", p=P)), (bouta[:, :], row(t["bout"], D)),
                     (router[:, :], t["router_w"]), (qkvw[:, :], t["qkv_w"]), (geow[:, :], t["kv_geo_w"]),
                     (kv_bias[:, 0:2 * D], row(t["qkv_b"], 2 * D, D)), (wob[:, 0, :], t["out_w"]), (boutb[:, :], row(t["out_b"], D)),
                     (kv_gate[:, :], bass.AP(tensor=t["kv_gate"].tensor, offset=0, ap=[[0, P], [1, 1]])),
                     (scale_row[:, :], row(t["mem_scale"], B_HEADS))]
                    + [(w_geo[:, i, :], t[k]) for i, k in enumerate(("w1_write", "w1_read", "w2_write", "w2_read"))]
                ):
                    sp.dma_start(dst, src).then_inc(late, 16)
                sp.wait_ge(zeroed, 2)
                sp.dma_start(bass.AP(tensor=xe_dram, offset=0, ap=[[D, P], [P * D, TILES], [1, D]]), zero[:, :, :]).then_inc(zfill, 16)
                sp.dma_start(bass.AP(tensor=ye_dram, offset=SLOTS * D, ap=[[D, P], [P * D, TILES], [1, D]]), zero[:, :, :]).then_inc(zfill, 16)
                sp.wait_ge(g_ready, 1)
                sp.dma_start(by_dist_dram[:, :], g_sb[:, :]).then_inc(g_stored, 16)
                sp.wait_ge(g_stored, 16)
                sp.dma_start(bias_dram[:, :].rearrange("(h p) w -> h p w", p=P),
                             bass.AP(tensor=by_dist_dram, offset=P - 1, ap=[[BIAS_M, A_HEADS], [-1, P], [1, BIAS_W]])
                             ).then_inc(g_stored, 16)
                sp.wait_ge(g_stored, 32)
                sp.wait_ge(zfill, 32)
                sp.wait_ge(late, 16 * LATE)

            @block.scalar
            def _(act):
                for h in range(ROWS // B_HEADS):
                    act.dma_start(dec_in[h * B_HEADS:(h + 1) * B_HEADS, :], t["decay_logits"].rearrange("(h a) -> h a", a=1)).then_inc(decays, 16)
                for a in range(GRP):
                    for r in range(REP):
                        act.dma_start(q_bias[a * 32 + r * B_DH:a * 32 + (r + 1) * B_DH, :],
                                      bass.AP(tensor=t["qkv_b"].tensor, offset=a * B_DH, ap=[[1, B_DH], [GRP * B_DH, B_HEADS // GRP]]), allow_slow_non_contiguous=True
                                      ).then_inc(one_row, 16)
                for f in range(FB):
                    act.dma_start(b1T[:, f, :], t["b1"][:, f * P:(f + 1) * P].rearrange("e p -> p e"), allow_slow_non_contiguous=True).then_inc(one_row, 16)
                act.wait_ge(decays, 16 * (ROWS // B_HEADS))
                nc.scalar.activation(dec_e[0:ROWS, :], dec_in[0:ROWS, :], ACT.Exp, scale=-1.0).then_inc(decays, 1)
                act.wait_ge(one_row, 16 * (GRP * REP + FB))

            @block.tensor
            def _(pe):
                pe.wait_ge(loaded, 32)
                pe.wait_ge(zeroed, 2)
                lo, hi = COLS["bucket"]
                nc.tensor.matmul(g_ps[0:A_HEADS, 0:BIAS_M], rel[:, :], tab[0:BUCKETS + 1, lo:hi], start=True, stop=True).then_inc(g_done, 1)

            @block.vector
            def _(dve):
                nc.vector.memset(rel[BUCKETS:BUCKETS + 1, :], 1.0).then_inc(zeroed, 1)
                nc.vector.memset(zero[:, :, :], 0.0).then_inc(zeroed, 1)
                nc.vector.memset(kv_bias[:, 2 * D:], 0.0)
                dve.wait_ge(g_done, 1)
                nc.vector.tensor_copy(g_sb[:, :], g_ps[0:A_HEADS, 0:BIAS_M]).then_inc(g_ready, 1)
                nc.vector.tensor_copy(upper_bf[:, :], col["upper"])
                nc.vector.tensor_copy(ones_bf[:, :], col["ones"])
                dve.wait_ge(decays, 16 * (ROWS // B_HEADS) + 1)
                nc.vector.tensor_scalar(dec_e[0:ROWS, :], dec_e[0:ROWS, :], 1.0, None, ALU.add).then_inc(g_ready, 1)
                dve.wait_ge(g_ready, 2)
                nc.vector.reciprocal(decay[0:ROWS, :], dec_e[0:ROWS, :])

            @block.gpsimd
            def _(pool):
                pool.wait_ge(late, 16 * LATE)
                nc.gpsimd.tensor_copy(w_kv[:, 0:2 * D], qkvw[:, D:])
                nc.gpsimd.tensor_copy(w_kv[:, 2 * D:], geow[:, :])
                nc.gpsimd.tensor_copy(w_q[:, :, :].rearrange("p g (a r d) -> p (g a) r d", a=GRP, r=REP),
                                      qkvw[:, 0:D].rearrange("p (h d) -> p h d", h=B_HEADS).unsqueeze(2).to_broadcast([P, B_HEADS, REP, B_DH]))

        def moe(name):
            layernorm(nc, name + "_ln", X, xn, xnT, ident)
            route(nc, name + "_route", xnT, router,
                  (upper_bf, ones_bf) + tuple(col[k].rearrange("p (t e) -> p t e", t=TILES) for k in ("prio", "ebase")) + (col["spare"],),
                  slot, gate)
            experts(nc, name + "_experts", xn, X, slot, gate, b1T, t["b2"], t["w1"], t["w2"], xe_dram, ye_dram, ident, col["ones"])

        layernorm(nc, "a_ln", X, xn, xnT, ident)
        with ExitStack() as a:
            KH, KL = (a.enter_context(nc.sbuf_tensor(n, [P, TOK], F32R)) for n in ("KH", "KL"))
            Vd = a.enter_context(nc.sbuf_tensor("Vd", [P, TILES, P], F32))
            O = a.enter_context(nc.sbuf_tensor("O", [P, TILES, A_HEADS * A_DH], F32))
            QS = [a.enter_context(nc.sbuf_tensor(f"QSa{i}", [P, SEQ], F32R)) for i in range(2)]
            prepare_a(nc, xnT, wkv[:, :, :, :].rearrange("p a b d -> p a (b d)"), KH, KL, Vd)
            attention(nc, "attn_a", True, 2, (KH, KL), Vd, O, QS, ident, None, xnT, t["Wq"], bias_dram, None, None)
            project_out(nc, "out_a", O, A_HEADS * A_DH // P, woa, bouta, X, ident)
        moe("moe1")
        layernorm(nc, "b_ln", X, xn, xnT, ident)
        with ExitStack() as a:
            gate_b = a.enter_context(nc.sbuf_tensor("gate_b", [P, TILES, B_HEADS], F32))
            geometry(nc, xnT, w_geo[:, :, :].rearrange("p a b -> p (a b)"), col["sel"].rearrange("p (g h) -> p g h", g=3),
                     decay, scale_row, kv_gate, gate_b, ident)
            QS4, KS4 = (a.enter_context(nc.sbuf_tensor(n, [P, B_HEADS // GRP, TOK], F32R)) for n in ("QS4", "KS4"))
            Vb = a.enter_context(nc.sbuf_tensor("Vb", [P, TILES, D], F32))
            O = a.enter_context(nc.sbuf_tensor("Ob", [P, TILES, D], F32))
            lo = COLS["low"][0]
            prepare_b(nc, xnT, w_kv, kv_bias, w_q, q_bias, gate_b, QS4, KS4, Vb, col["sign"],
                      tab[:, lo:lo + 1], tab[:, lo + 1:lo + 2], ident)
            QS = [a.enter_context(nc.sbuf_tensor(f"QSb{i}", [P, SEQ], F32R)) for i in range(2)]
            attention(nc, "attn_b", False, GRP, (KS4,), Vb, O, QS, ident, col["window"], None, None, None, QS4, col["hmask"])
            project_out(nc, "out_b", O, 1, wob, boutb, X, ident)
        moe("moe2")
        with Phase(nc, "store") as ph:
            stored = ph.sem("stored")
            block = ph.block()

            @block.sync
            def _(sp):
                sp.dma_start(out.rearrange("b (t p) d -> p (b t) d", p=P), X[:, :, :]).then_inc(stored, 16)
                sp.wait_ge(stored, 16)


def kernel(**inputs):
    import concourse.bacc as bacc
    from concourse.bass_utils import run_bass_kernel_spmd

    nc = bacc.Bacc("TRN2", target_bir_lowering=False, num_devices=1)
    arrays, args = {}, {}
    for name, a in list(inputs.items()) + [("table", tables())]:
        a = np.ascontiguousarray(a).reshape(np.shape(a) or (1,))
        key = f"in_{name}_dram"
        arrays[key] = a
        short = name
        for prefix in ("L0_attn_a_", "L0_attn_b_", "L0_ffn_"):
            short = short.removeprefix(prefix)
        args[short] = nc.dram_tensor(key, a.shape, mybir.dt.from_np(a.dtype), kind="ExternalInput").ap()
    out = nc.dram_tensor("out_0_dram", (BATCH, SEQ, D), F32, kind="ExternalOutput").ap()
    build(nc, args, out)
    r = run_bass_kernel_spmd(nc, [arrays], core_ids=[0])
    return r.results[0]["out_0_dram"]
```

```python
import numpy as np
import concourse.bass as bass
from concourse import mybir
from contextlib import ExitStack

F32 = mybir.dt.float32
F32R = mybir.dt.float32r
BF16 = mybir.dt.bfloat16
I32 = mybir.dt.int32
ALU = mybir.AluOpType
ACT = mybir.ActivationFunctionType
AX = mybir.AxisListType

P = 128
BATCH, SEQ, D = 2, 1024, 128
TOK = BATCH * SEQ
TILES = TOK // P
QT = SEQ // P
BANK = 512
BLK = BANK // P
ORDER = (4, 1, 5, 0, 6, 2, 7, 3)
EPS = 1e-5
MASKED = 1e30

A_HEADS, A_DH = 16, 64
BUCKETS, MAX_DIST = 32, 128
BIAS_W = 2 * P
BIAS_M = P + BIAS_W - 1
B_HEADS, B_DH = 16, 8
GRP = 4
REP = P // (GRP * B_DH)
PAIRS = 21
ROWS = 7 * B_HEADS
E, F, CAP = 8, 512, TOK // 8
FB = F // P
SLOTS = E * CAP


class Chain:

    def __init__(self, eng, sem):
        self.eng, self.sem, self.n = eng, sem, 0

    def __call__(self, ins):
        self.n += 1
        ins.then_inc(self.sem, 1)
        self.eng.wait_ge(self.sem, self.n)


class Phase:

    def __init__(self, nc, name):
        self.nc, self.name = nc, name

    def __enter__(self):
        self.ctx = ExitStack()
        return self

    def sem(self, name):
        return self.ctx.enter_context(self.nc.semaphore(f"{self.name}_{name}"))

    def psum(self, name, shape):
        return self.ctx.enter_context(self.nc.psum_tensor(f"{self.name}_{name}", shape, F32))

    def sb(self, name, shape, dt=F32):
        return self.ctx.enter_context(self.nc.sbuf_tensor(f"{self.name}_{name}", shape, dt))

    def block(self):
        return self.ctx.enter_context(self.nc.Block())

    def __exit__(self, *a):
        return self.ctx.__exit__(*a)


def layernorm(nc, name, X, xn, xnT, ident, router=None, logit=None):
    with Phase(nc, name) as ph:
        stats, mv = ph.sb("stats", [P, TILES, 6]), ph.sb("mv", [P, TILES, 2])
        var, dev, rstd = ph.sb("var", [P, TILES]), ph.sb("dev", [P, TILES]), ph.sb("rstd", [P, TILES])
        bank = [ph.psum(f"bank{i}", [P, BANK]) for i in range(TILES // BLK)]
        chain, var_ready, dev_ready = ph.sem("chain"), ph.sem("var_ready"), ph.sem("dev_ready")
        xn_ready, turned, copied = ph.sem("xn_ready"), ph.sem("turned"), ph.sem("copied")
        block = ph.block()

        @block.vector
        def _(dve):
            link = Chain(dve, chain)
            nc.vector.memset(xnT[:, :, 0:1], 0.0)
            for i in range(TILES):
                ins = nc.vector.bn_stats(stats[:, i, :], X[:, i, :])
            link(ins)
            for i in range(TILES):
                ins = nc.vector.bn_aggr(mv[:, i, :], stats[:, i, :])
            link(ins)
            nc.vector.tensor_scalar(var[:, :], mv[:, :, 1], EPS, None, ALU.add).then_inc(var_ready, 1)
            dve.wait_ge(dev_ready, 1)
            link(nc.vector.reciprocal(rstd[:, :], dev[:, :]))
            for i in range(TILES):
                nc.vector.tensor_scalar(xn[:, i, :], X[:, i, :], mv[:, i, 0:1], rstd[:, i:i + 1],
                                        ALU.subtract, ALU.mult).then_inc(xn_ready, 1)

        @block.scalar
        def _(act):
            act.wait_ge(var_ready, 1)
            nc.scalar.activation(dev[:, :], var[:, :], ACT.Sqrt).then_inc(dev_ready, 1)
            for g in range(TILES // BLK):
                act.wait_ge(turned, g + 1)
                b, at = g // (QT // BLK), 1 + (g % (QT // BLK)) * BANK
                nc.scalar.activation(xnT[:, b, at:at + BANK], bank[g][:, :], ACT.Copy).then_inc(copied, 1)

        @block.tensor
        def _(pe):
            for i in range(TILES):
                pe.wait_ge(xn_ready, i + 1)
                j = i % BLK
                ins = nc.tensor.transpose(bank[i // BLK][:, j * P:(j + 1) * P], xn[:, i, :], ident[:, :])
                if j == BLK - 1:
                    ins.then_inc(turned, 1)
            for i in range(TILES if router is not None else 0):
                if i % BLK == 0:
                    pe.wait_ge(copied, i // BLK + 1)
                at = 1 + (i % QT) * P
                nc.tensor.matmul(logit[:, i, :], xnT[:, i // QT, at:at + P], router[:, :], start=True, stop=True)





def attention(nc, name, is_a, hu, KS, V, O_all, QS, ident, window, xnT, wq_dram, bias_dram, QS4, hmask):
    heads = A_HEADS if is_a else B_HEADS
    OWN = [slice(0, A_DH), slice(A_DH, P)]
    dh = A_DH if is_a else B_DH
    its, S = heads // hu, QT * hu
    TC = sum(1 if qt < BLK else 2 for qt in range(QT)) * hu
    NSLOT, RING = 6, 8
    PROJ = SEQ // BANK if is_a else 0
    FIRST_MOVED = PROJ // 2 if is_a else 1
    uses = TC + PROJ * hu // 2
    win_max = BIAS_W if is_a else P
    scale = -(A_DH ** -0.5)
    assert TC % NSLOT == 0 and uses % 2 == 0 and S % RING == 0

    def tile(k):
        return ORDER[k % QT]

    def chunks(k):
        return range(1 if tile(k) < BLK else 2)

    def blocks(k, c):
        return range(c * BLK, min(tile(k) + 1, (c + 1) * BLK))

    def on_dve(k, c):
        return tile(k) < BLK or c == 1

    def prepares(k, last):
        return is_a and k % (2 * QT) == QT + 1 and not (last and k // QT == hu - 1)

    def numbering(last):
        t, p, n = {}, {}, 0
        for k in range(S):
            for c in chunks(k):
                t[k, c], n = n, n + 1
            if prepares(k, last):
                for c in range(PROJ):
                    p[k // QT, c], n = n, n + 1
        return t, p

    chunk_no = {kc: i for i, kc in enumerate((k, c) for k in range(S) for c in chunks(k))}
    far_no = {j: i for i, j in enumerate(j for j in range(S) if P * (tile(j) + 1) > win_max)}

    with Phase(nc, name) as ph:
        score = [ph.psum(f"score{i}", [P, 2 * BANK]) for i in range(2)]
        pt = [ph.psum(f"pt{i}", [P, BANK]) for i in range(2)]
        o_ps = [ph.psum(f"o{i}", [P, BANK]) for i in range(2)]
        prob = [ph.sb(f"prob{i}", [P, SEQ]) for i in range(4)]
        pts = [ph.sb(f"pts{i}", [P, BANK]) for i in range(NSLOT)]
        m_far, m_all = ph.sb("m_far", [P, RING]), ph.sb("m_all", [P, RING])
        scratch, pool_scratch = ph.sb("scratch", [P, 1]), ph.sb("pool_scratch", [P, 1])
        rowsum, rinv = ph.sb("rowsum", [P, RING]), ph.sb("rinv", [P, RING])
        qk_done, max_done, exp_done = ph.sem("qk_done"), ph.sem("max_done"), ph.sem("exp_done")
        far_done, inv_done = ph.sem("far_done"), ph.sem("inv_done")
        pt_done, slot_free, o_free = ph.sem("pt_done"), ph.sem("slot_free"), ph.sem("o_free")
        moved = [ph.sem(f"moved{i}") for i in range(2)]
        qs_ready, hi_done = ph.sem("qs_ready"), ph.sem("hi_done")
        placed, pool_placed = ph.sem("placed"), ph.sem("pool_placed")
        if is_a:
            wq = [ph.sb(f"wq{i}", [P, 2 * A_DH]) for i in range(2)]
            bt = [ph.sb(f"bt{i}", [P, BIAS_W]) for i in range(2)]
            wq_ready = [ph.sem(f"wq_ready{i}") for i in range(2)]
            bt_ready = [ph.sem(f"bt_ready{i}") for i in range(2)]
        block = ph.block()

        def halves(it, n):
            return it * (uses // 2) + FIRST_MOVED + n // 2

        def loads(it, u):
            return (it * (hu // 2) + u // 2 + 1) * 16

        def run(eng, start, body):
            for b in range(BATCH):
                start(b)
                with eng.Fori(0, its - 1) as i:
                    body(b, i + b * its, i, False)
                body(b, b * its + its - 1, its - 1, True)

        @block.tensor
        def _(pe):
            pe.sem_inc(slot_free, NSLOT)
            if not is_a:
                for sem in moved:
                    pe.sem_inc(sem, FIRST_MOVED)

            def project(b, it, u, n0):
                pair = u // 2 % 2
                pe.wait_ge(wq_ready[pair], (it + u // hu + 1) * 16)
                for c in range(PROJ):
                    if n0 is not None:
                        pe.wait_ge(moved[(n0[1] + c) % 2], n0[0] + (n0[1] + c) // 2)
                    bank = pt[c if n0 is None else (n0[1] + c) % 2]
                    nc.tensor.matmul(bank[:, :], wq[pair][:, :], xnT[:, b, 1 + c * BANK:1 + (c + 1) * BANK],
                                     start=True, stop=True).then_inc(pt_done, 1)

            def scores(b, itl, j, ready):
                u, qt = j // QT, tile(j)
                if ready is not None:
                    for sem, value in ready:
                        pe.wait_ge(sem, value)
                for c0 in range(0, P * (qt + 1), BANK):
                    w = max(min(BANK, P * (qt + 1) - c0), 2 * P)
                    at = b * SEQ + c0
                    parts = [k[:, at:at + w] for k in KS] if is_a else [KS[0][:, itl, at:at + w]]
                    for n, part in enumerate(parts):
                        ins = nc.tensor.matmul(score[j % 2][:, c0:c0 + w], QS[u % len(QS)][:, qt * P:(qt + 1) * P],
                                               part, start=n == 0, stop=n == len(parts) - 1)
                ins.then_inc(qk_done, 1)

            def ready_after(it, u, p_no):
                if is_a:
                    if u % 2 == 0:
                        return None
                    return [(moved[p_no[u, c] % 2], halves(it, p_no[u, c]) + 1) for c in range(PROJ)]
                return [(qs_ready, it * hu + u + 2)]

            def start(b):
                if is_a:
                    project(b, b * its, 0, None if b == 0 else (b * its * uses // 2, 0))
                    ready = [(moved[c], b * its * uses // 2 + 1) for c in range(PROJ)]
                else:
                    ready = [(qs_ready, b * its * hu + 1)]
                scores(b, 0, 0, ready)
                scores(b, 0, 1, None)

            def body(b, it, itl, last):
                t_no, p_no = numbering(last)

                def output(k):
                    pe.wait_ge(o_free, it * S + k + 1)
                    for c in chunks(k):
                        n, i = t_no[k, c], chunk_no[k, c]
                        pe.wait_ge(moved[n % 2], halves(it, n) + 1)
                        for blk in blocks(k, c):
                            ins = nc.tensor.matmul(o_ps[k % 2][:, 0:P],
                                                   pts[i % NSLOT][:, (blk % BLK) * P:(blk % BLK + 1) * P],
                                                   V[:, b * QT + blk, :], start=blk == 0, stop=blk == tile(k))
                        ins.then_inc(slot_free, 1)

                for k in range(S):
                    pe.wait_ge(exp_done, it * S + k + 1)
                    if k + 2 < S:
                        scores(b, itl, k + 2, ready_after(it, (k + 2) // QT - 1, p_no) if (k + 2) % QT == 0 else None)
                    elif not last:
                        scores(b, itl + 1, k + 2 - S, ready_after(it, hu - 1, p_no))
                    for c in chunks(k):
                        n = t_no[k, c]
                        pe.wait_ge(moved[n % 2], halves(it, n))
                        for blk in blocks(k, c):
                            ins = nc.tensor.transpose(pt[n % 2][:, (blk % BLK) * P:(blk % BLK + 1) * P],
                                                      prob[k % 4][:, blk * P:(blk + 1) * P], ident[:, :])
                        ins.then_inc(pt_done, 1)
                    if prepares(k, last):
                        u = k // QT
                        project(b, it, u + 1, (halves(it, 0), p_no[u, 0]))
                    if k > 0:
                        output(k - 1)
                output(S - 1)

            run(pe, start, body)

        @block.vector
        def _(dve):
            dve.sem_inc(o_free, 2)

            def row_max(it, j, between):
                u, qt, r = j // QT, tile(j), j % RING
                nk = P * (qt + 1)
                win = min(nk, win_max)
                least = 3e38
                table = window
                if is_a:
                    table = bt[u % 2][:, BIAS_W - win:BIAS_W]
                if is_a and j % QT == 0:
                    dve.wait_ge(bt_ready[u % 2], loads(it, u))
                if nk > win:
                    dve.wait_ge(qk_done, it * S + j + 1)
                    least = m_far[:, r:r + 1]
                    nc.vector.tensor_reduce(least, score[j % 2][:, 0:nk - win], AX.X, ALU.min).then_inc(far_done, 1)
                    dve.wait_ge(far_done, it * len(far_no) + far_no[j] + 1)
                else:
                    dve.wait_ge(qk_done, it * S + j + 1)
                between()
                near = score[j % 2][:, nk - win:nk]
                nc.vector.tensor_tensor_reduce(out=near, in0=near, in1=table, scale=1.0, scalar=least,
                                               op0=ALU.add, op1=ALU.min,
                                               accum_out=m_all[:, r:r + 1]).then_inc(max_done, 1)

            def place(n):
                if n:
                    dve.wait_ge(placed, n)
                nc.vector.memset(scratch[:, :], 0.0).then_inc(placed, 1)

            def invert(it, k):
                r = k % RING
                dve.wait_ge(exp_done, it * S + k + 1)
                nc.vector.reciprocal(rinv[:, r:r + 1], rowsum[:, r:r + 1]).then_inc(inv_done, 1)

            def norm(b, it, itl, k):
                r = k % RING
                i = chunk_no[k, chunks(k)[-1]]
                dve.wait_ge(slot_free, it * TC + NSLOT + i + 1)
                dve.wait_ge(inv_done, it * S + k + 1)
                at = (itl * hu + k // QT) * dh
                src = o_ps[k % 2][:, 0:dh] if is_a else o_ps[k % 2][:, bass.ds(at, dh)]
                nc.vector.tensor_scalar(O_all[:, b * QT + tile(k), bass.ds(at, dh)], src, rinv[:, r:r + 1],
                                        None, ALU.mult).then_inc(o_free, 1)

            def low_parts(pair, u, first):
                for c in range(PROJ):
                    dve.wait_ge(hi_done, pair * PROJ + c + 1)
                    bank, cols = (first + c) % 2, slice(c * BANK, (c + 1) * BANK)
                    for half in range(2):
                        own, other = OWN[half], OWN[1 - half]
                        ins = nc.vector.scalar_tensor_tensor(QS[(u + half) % hu][other, cols], pt[bank][own, :], scale,
                                                             QS[(u + half) % hu][own, cols].bitcast(F32),
                                                             ALU.mult, ALU.subtract)
                    ins.then_inc(moved[bank], 1)

            def start(b):
                if is_a:
                    low_parts(b * heads // 2, 0, 0)
                for j in range(2):
                    row_max(b * its, j, lambda: place(2 * b + j))

            def body(b, it, itl, last):
                t_no, p_no = numbering(last)
                for k in range(S):
                    if k + 2 < S:
                        row_max(it, k + 2, lambda: invert(it, k))
                    elif not last:
                        row_max(it + 1, k + 2 - S, lambda: invert(it, k))
                    else:
                        invert(it, k)
                    for c in chunks(k):
                        if on_dve(k, c):
                            n, i, w = t_no[k, c], chunk_no[k, c], P * len(blocks(k, c))
                            dve.wait_ge(pt_done, it * uses + PROJ + n + 1)
                            dve.wait_ge(slot_free, it * TC + i + 1)
                            nc.vector.tensor_copy(pts[i % NSLOT][:, 0:w], pt[n % 2][:, 0:w]).then_inc(moved[n % 2], 1)
                    if k > 0:
                        norm(b, it, itl, k - 1)
                    if prepares(k, last):
                        u = k // QT
                        low_parts(it * (hu // 2) + (u + 1) // 2, u + 1, p_no[u, 0])
                norm(b, it, itl, S - 1)

            run(dve, start, body)

        @block.scalar
        def _(act):
            def exp(it, j):
                r, nk = j % RING, P * (tile(j) + 1)
                act.wait_ge(max_done, it * S + j + 1)
                nc.scalar.activation(prob[j % 4][:, 0:nk], score[j % 2][:, 0:nk], ACT.Exp, bias=m_all[:, r:r + 1],
                                     scale=-1.0, accum_out=rowsum[:, r:r + 1]).then_inc(exp_done, 1)

            def high_parts(u, first, use):
                for c in range(PROJ):
                    act.wait_ge(pt_done, use + c + 1)
                    for half in range(2):
                        ins = nc.scalar.activation(QS[(u + half) % hu][OWN[half], c * BANK:(c + 1) * BANK],
                                                   pt[(first + c) % 2][OWN[half], :], ACT.Copy, scale=scale)
                    ins.then_inc(hi_done, 1)

            def start(b):
                if is_a:
                    high_parts(0, 0, b * its * uses)
                exp(b * its, 0)

            def body(b, it, itl, last):
                t_no, p_no = numbering(last)
                for k in range(S):
                    if k + 1 < S:
                        exp(it, k + 1)
                    elif not last:
                        exp(it + 1, 0)
                    for c in chunks(k):
                        if not on_dve(k, c):
                            n, i, w = t_no[k, c], chunk_no[k, c], P * len(blocks(k, c))
                            act.wait_ge(pt_done, it * uses + PROJ + n + 1)
                            act.wait_ge(slot_free, it * TC + i + 1)
                            nc.scalar.activation(pts[i % NSLOT][:, 0:w], pt[n % 2][:, 0:w], ACT.Copy).then_inc(moved[n % 2], 1)
                    if prepares(k, last):
                        u = k // QT
                        high_parts(u + 1, p_no[u, 0], it * uses + PROJ + p_no[u, 0])

            run(act, start, body)

        if is_a:
            @block.sync
            def _(sp):
                def load(head, u):
                    sp.dma_start(bt[u % 2][:, :], bias_dram[bass.ds(head * P, P), :]).then_inc(bt_ready[u % 2], 16)

                def load_weights(head, u):
                    sp.dma_start(wq[u // 2 % 2][:, :], bass.AP(tensor=wq_dram.tensor, offset=head * A_DH,
                                                               ap=[[A_HEADS * A_DH, P], [1, 2 * A_DH]])
                                 ).then_inc(wq_ready[u // 2 % 2], 16)

                def start(b):
                    if b == 0:
                        load_weights(0, 0)
                        load(0, 0)

                def body(b, it, itl, last):
                    for u in range(hu):
                        if last and u == hu - 1 and b == BATCH - 1:
                            continue
                        sp.wait_ge(max_done, it * S + u * QT + 1)
                        wrap = last and u == hu - 2
                        if u % 2 == 0 and not (wrap and b == BATCH - 1):
                            load_weights(0 if wrap else itl * hu + u + 2, u + 2)
                        load(0 if last and u == hu - 1 else itl * hu + u + 1, u + 1)

                run(sp, start, body)
        else:
            @block.gpsimd
            def _(pool):
                def queries(b, itl, u, value, turn=None):
                    if turn is not None:
                        pool.wait_ge(pool_placed, turn)
                    if value is not None:
                        pool.wait_ge(qk_done, value)
                    nc.gpsimd.tensor_tensor(pool_scratch[:, :], hmask[:, 0:1], hmask[:, 0:1],
                                            ALU.mult).then_inc(pool_placed, 1)
                    nc.gpsimd.tensor_tensor(QS[u % 2][:, :], QS4[:, itl, b * SEQ:(b + 1) * SEQ].bitcast(F32),
                                            hmask[:, u % GRP:u % GRP + 1].to_broadcast([P, SEQ]),
                                            ALU.mult).then_inc(qs_ready, 1)

                def start(b):
                    queries(b, 0, 0, b * its * S if b else None, b * its * hu if b else None)

                def body(b, it, itl, last):
                    for u in range(hu):
                        if u + 1 < hu:
                            queries(b, itl, u + 1, (it * hu + u) * QT + 1, it * hu + u + 1)
                        elif not last:
                            queries(b, itl + 1, 0, (it * hu + u) * QT + 1, it * hu + u + 1)

                run(pool, start, body)


def project_out(nc, name, O_all, blocks, w_out, bias, X, ident):
    with Phase(nc, name) as ph:
        pt = [ph.psum(f"pt{i}", [P, BANK]) for i in range(4)]
        y_ps = [ph.psum(f"y{i}", [P, BANK]) for i in range(2)]
        oT = [ph.sb(f"oT{i}", [P, blocks, P]) for i in range(2)]
        turned, y_done, y_used = ph.sem("turned"), ph.sem("y_done"), ph.sem("y_used")
        moved_act, biased = ph.sem("moved_act"), ph.sem("biased")
        block = ph.block()
        per = (blocks + BLK - 1) // BLK

        def part(c):
            return range(c * BLK, min(blocks, (c + 1) * BLK))

        @block.tensor
        def _(pe):
            def turn(i):
                for c in range(per):
                    n = i * per + c
                    if n >= 4:
                        pe.wait_ge(moved_act, n - 3)
                    for j in part(c):
                        ins = nc.tensor.transpose(pt[n % 4][:, (j % BLK) * P:(j % BLK + 1) * P],
                                                  O_all[:, i, j * P:(j + 1) * P], ident[:, :])
                    ins.then_inc(turned, 1)

            turn(0)
            for i in range(TILES):
                if i + 1 < TILES:
                    turn(i + 1)
                pe.wait_ge(moved_act, (i + 1) * per)
                if i >= 2:
                    pe.wait_ge(y_used, i - 1)
                for j in range(blocks):
                    ins = nc.tensor.matmul(y_ps[i % 2][:, 0:P], oT[i % 2][:, j, :], w_out[:, j, :],
                                           start=j == 0, stop=j == blocks - 1)
                ins.then_inc(y_done, 1)

        @block.scalar
        def _(act):
            for i in range(TILES):
                if i >= 2:
                    act.wait_ge(y_done, i - 1)
                for c in range(per):
                    act.wait_ge(turned, i * per + c + 1)
                    w = P * len(part(c))
                    nc.scalar.activation(oT[i % 2][:, c * BLK:c * BLK + len(part(c)), :].rearrange("p j q -> p (j q)"),
                                         pt[(i * per + c) % 4][:, 0:w], ACT.Copy).then_inc(moved_act, 1)

        @block.vector
        def _(dve):
            nc.vector.tensor_tensor(X[:, :, :], X[:, :, :], bias[:, :].unsqueeze(1).to_broadcast([P, TILES, D]),
                                    ALU.add).then_inc(biased, 1)
            dve.wait_ge(biased, 1)
            for i in range(TILES):
                dve.wait_ge(y_done, i + 1)
                nc.vector.tensor_tensor(X[:, i, :], X[:, i, :], y_ps[i % 2][:, 0:D], ALU.add).then_inc(y_used, 1)


def prepare_a(nc, xnT, wkv, KH, KL, Vd):
    with Phase(nc, "prep_a") as ph:
        kp = [ph.psum(f"k{i}", [P, BANK]) for i in range(4)]
        vp = [ph.psum(f"v{i}", [P, BANK]) for i in range(4)]
        k_done, v_done, high = ph.sem("k_done"), ph.sem("v_done"), ph.sem("high")
        block = ph.block()

        @block.tensor
        def _(pe):
            for g in range(4):
                b, at = g // 2, 1 + (g % 2) * BANK
                nc.tensor.matmul(kp[g][:, :], wkv[:, 0, :], xnT[:, b, at:at + BANK],
                                 start=True, stop=True).then_inc(k_done, 1)
            for i in range(TILES):
                at = 1 + (i % QT) * P
                ins = nc.tensor.matmul(vp[i // BLK][:, (i % BLK) * P:(i % BLK + 1) * P],
                                       xnT[:, i // QT, at:at + P], wkv[:, 1, :], start=True, stop=True)
                if i % BLK == BLK - 1:
                    ins.then_inc(v_done, 1)

        @block.scalar
        def _(act):
            for g in range(4):
                act.wait_ge(k_done, g + 1)
                nc.scalar.activation(KH[:, g * BANK:(g + 1) * BANK], kp[g][:, :], ACT.Copy).then_inc(high, 1)
            for g in range(4):
                act.wait_ge(v_done, g + 1)
                nc.scalar.activation(Vd[:, g * BLK:(g + 1) * BLK, :].rearrange("p t d -> p (t d)"), vp[g][:, :], ACT.Copy)

        @block.vector
        def _(dve):
            for g in range(4):
                dve.wait_ge(high, g + 1)
                nc.vector.tensor_tensor(KL[:, g * BANK:(g + 1) * BANK], kp[g][:, :],
                                        KH[:, g * BANK:(g + 1) * BANK].bitcast(F32), ALU.subtract)


def route(nc, name, logit, consts, slot, gate):
    upper, ones_bf, prio, ebase, spare = consts
    with Phase(nc, name) as ph:
        count, total = (ph.psum(n, [P, BANK // E, E])[:, 0:TILES, :] for n in ("count", "total"))
        a, ex, mask = ph.sb("a", [P, TILES, E]), ph.sb("ex", [P, TILES, E]), ph.sb("mask", [P, TILES, E])
        mask_bf = ph.sb("mask_bf", [P, TILES, E], BF16)
        tot, run, one = ph.sb("tot", [P, TILES, E]), ph.sb("run", [P, TILES, E]), ph.sb("one", [P, TILES])
        m1, m2, pos = ph.sb("m1", [P, TILES]), ph.sb("m2", [P, TILES]), ph.sb("pos", [P, TILES])
        keep, row = ph.sb("keep", [P, TILES]), ph.sb("row", [P, TILES])
        chain, shifted, exped = ph.sem("chain"), ph.sem("shifted"), ph.sem("exped")
        masked, counted = ph.sem("masked"), ph.sem("counted")
        block = ph.block()

        def wide(x):
            return x[:, :].unsqueeze(2).to_broadcast([P, TILES, E])

        @block.tensor
        def _(pe):
            pe.wait_ge(masked, 1)
            flat = mask_bf[:, :, :].rearrange("p t e -> p (t e)")
            nc.tensor.matmul(count[:, :, :].rearrange("p t e -> p (t e)"), upper[:, :], flat, start=True, stop=True)
            nc.tensor.matmul(total[:, :, :].rearrange("p t e -> p (t e)"), ones_bf[:, :], flat,
                             start=True, stop=True).then_inc(counted, 1)

        @block.scalar
        def _(act):
            act.wait_ge(shifted, 1)
            nc.scalar.activation(ex[:, :, :], a[:, :, :], ACT.Exp).then_inc(exped, 1)

        @block.vector
        def _(dve):
            link = Chain(dve, chain)
            nc.vector.memset(one[:, :], 1.0)
            link(nc.vector.tensor_reduce(m1[:, :], logit[:, :, :], AX.X, ALU.max))
            nc.vector.tensor_tensor(a[:, :, :], logit[:, :, :], wide(m1), ALU.subtract).then_inc(shifted, 1)
            dve.wait_ge(exped, 1)
            link(nc.vector.tensor_reduce(m2[:, :], ex[:, :, :], AX.X, ALU.add))
            link(nc.vector.tensor_reduce(m1[:, :], ex[:, :, :], AX.X, ALU.max))
            link(nc.vector.reciprocal(keep[:, :], m2[:, :]))
            link(nc.vector.tensor_tensor(gate[:, :], m1[:, :], keep[:, :], ALU.mult))
            link(nc.vector.tensor_tensor(a[:, :, :], ex[:, :, :], wide(m1), ALU.is_equal))
            link(nc.vector.tensor_tensor(a[:, :, :], a[:, :, :], prio[:, :, :], ALU.mult))
            link(nc.vector.tensor_reduce(m2[:, :], a[:, :, :], AX.X, ALU.max))
            link(nc.vector.tensor_tensor(mask[:, :, :], a[:, :, :], wide(m2), ALU.is_equal))
            nc.vector.tensor_copy(mask_bf[:, :, :], mask[:, :, :]).then_inc(masked, 1)
            dve.wait_ge(counted, 1)
            link(nc.vector.tensor_copy(tot[:, :, :], total[:, :, :]))
            for e in range(E):
                ins = nc.vector.tensor_tensor_scan(run[:, :, e], one[:, :], tot[:, :, e], 0.0, ALU.mult, ALU.add)
            link(ins)
            link(nc.vector.tensor_tensor(run[:, :, :], run[:, :, :], tot[:, :, :], ALU.subtract))
            link(nc.vector.tensor_tensor(run[:, :, :], run[:, :, :], count[:, :, :], ALU.add))
            link(nc.vector.tensor_tensor(run[:, :, :], run[:, :, :], mask[:, :, :], ALU.mult))
            link(nc.vector.tensor_reduce(pos[:, :], run[:, :, :], AX.X, ALU.add))
            link(nc.vector.tensor_tensor(a[:, :, :], mask[:, :, :], ebase[:, :, :], ALU.mult))
            link(nc.vector.tensor_reduce(row[:, :], a[:, :, :], AX.X, ALU.add))
            link(nc.vector.tensor_scalar(keep[:, :], pos[:, :], float(CAP), None, ALU.is_le))
            link(nc.vector.tensor_tensor(row[:, :], row[:, :], pos[:, :], ALU.add))
            link(nc.vector.tensor_tensor(row[:, :], row[:, :], spare[:, :], ALU.subtract))
            link(nc.vector.tensor_tensor(row[:, :], row[:, :], keep[:, :], ALU.mult))
            link(nc.vector.tensor_tensor(row[:, :], row[:, :], spare[:, :], ALU.add))
            nc.vector.tensor_scalar(slot[:, :], row[:, :], -1.0, None, ALU.add)


def experts(nc, name, xn, X, slot, gate, b1T, b2_dram, w1_dram, w2_dram, xe_dram, ye_dram, ident):
    with Phase(nc, name) as ph:
        NW = 2
        w1 = [ph.sb(f"w1_{i}", [P, F]) for i in range(NW)]
        w2 = [ph.sb(f"w2_{i}", [P, FB, D]) for i in range(NW)]
        b2 = [ph.sb(f"b2_{i}", [P, D]) for i in range(NW)]
        xe = [ph.sb(f"xe{i}", [P, 2, D]) for i in range(NW)]
        xeT = [ph.sb(f"xeT{i}", [P, CAP]) for i in range(NW)]
        hT = [ph.sb(f"hT{i}", [P, FB, CAP]) for i in range(NW)]
        ye = [ph.sb(f"ye{i}", [P, 2, D]) for i in range(NW)]
        back = ph.sb("back", [P, TILES, D])
        t_ps = [ph.psum(f"t{i}", [P, BANK])[:, 0:CAP] for i in range(2)]
        h_ps = [ph.psum(f"h{i}", [P, 2, CAP]) for i in range(4)]
        y_ps = [ph.psum(f"y{i}", [P, BLK, D])[:, 0:2, :] for i in range(2)]
        sent = ph.sem("sent")
        w1_ready, w2_ready = [ph.sem(f"w1_ready{i}") for i in range(NW)], [ph.sem(f"w2_ready{i}") for i in range(NW)]
        xe_ready = [ph.sem(f"xe_ready{i}") for i in range(NW)]
        turned, xeT_ready, h_done = ph.sem("turned"), ph.sem("xeT_ready"), ph.sem("h_done")
        relu_act, relu_dve, y_done, ye_ready = ph.sem("relu_act"), ph.sem("relu_dve"), ph.sem("y_done"), ph.sem("ye_ready")
        stored = [ph.sem(f"stored{i}") for i in range(NW)]
        fetched = [ph.sem(f"fetched{i}") for i in range(TILES // BLK)]
        block = ph.block()
        ITS = E // NW

        def first_layer(eng, e, i):
            eng.dma_start(w1[i][:, :], bass.AP(tensor=w1_dram.tensor, offset=e * (D * F), ap=[[F, P], [1, F]])).then_inc(w1_ready[i], 16)

        @block.gpsimd
        def _(pool):
            for i in range(TILES):
                pool.indirect_dma_start(out=xe_dram[:, :], out_offset=bass.IndirectOffsetOnAxis(ap=slot[:, i:i + 1], axis=0),
                                        in_=xn[:, i, :], in_offset=None).then_inc(sent, 16)

            def rows(e, i):
                pool.dma_start(xe[i][:, :, :], bass.AP(tensor=xe_dram, offset=e * (CAP * D),
                                                       ap=[[D, P], [P * D, 2], [1, D]])).then_inc(xe_ready[i], 16)

            pool.wait_ge(sent, 16 * TILES)
            for i in range(NW):
                rows(i, i)
            with pool.Fori(0, ITS - 1) as it:
                for i in range(NW):
                    pool.wait_ge(turned, it * NW + i + 1)
                    rows((it + 1) * NW + i, i)
            for i in range(NW):
                pool.wait_ge(stored[i], 16 * (ITS + 1))
            for i in range(TILES):
                pool.indirect_dma_start(out=back[:, i, :], out_offset=None, in_=ye_dram[:, :],
                                        in_offset=bass.IndirectOffsetOnAxis(ap=slot[:, i:i + 1], axis=0)).then_inc(fetched[i // BLK], 16)

        @block.sync
        def _(sp):
            def second_layer(e, i):
                sp.dma_start(w2[i][:, :, :], bass.AP(tensor=w2_dram.tensor, offset=e * (F * D),
                                                     ap=[[D, P], [P * D, FB], [1, D]])).then_inc(w2_ready[i], 16)
                sp.dma_start(b2[i][:, :], bass.AP(tensor=b2_dram.tensor, offset=e * D, ap=[[0, P], [1, D]])).then_inc(w2_ready[i], 16)

            for i in range(NW):
                first_layer(sp, i, i)
                second_layer(i, i)
            def body(it, last):
                for i in range(NW):
                    n = it * NW + i
                    if not last:
                        sp.wait_ge(ye_ready, n + 2)
                        second_layer((it + 1) * NW + i, i)
                    sp.wait_ge(ye_ready, n + 2)
                    sp.dma_start(bass.AP(tensor=ye_dram, offset=n * (CAP * D),
                                         ap=[[D, P], [P * D, 2], [1, D]]), ye[i][:, :, :]).then_inc(stored[i], 16)

            with sp.Fori(0, ITS - 1) as it:
                body(it, False)
            body(ITS - 1, True)

        @block.tensor
        def _(pe):
            for sem in (xeT_ready, ye_ready):
                pe.sem_inc(sem, 1)
            for sem in (relu_act, relu_dve):
                pe.sem_inc(sem, 2)
            for sem in stored:
                pe.sem_inc(sem, 16)

            def turn(it, i):
                n = it * NW + i
                pe.wait_ge(xe_ready[i], (it + 1) * 16)
                if not (isinstance(it, int) and it == 0):
                    pe.wait_ge(xeT_ready, n)
                for c in range(2):
                    ins = nc.tensor.transpose(t_ps[i][:, c * P:(c + 1) * P], xe[i][:, c, :], ident[:, :])
                ins.then_inc(turned, 1)

            def first(it, i):
                n = it * NW + i
                pe.wait_ge(xeT_ready, n + 2)
                pe.wait_ge(w1_ready[i], (it + 1) * 16)
                pe.wait_ge(relu_act, n + 1)
                pe.wait_ge(relu_dve, n + 1)
                for f in range(FB):
                    ins = nc.tensor.matmul(h_ps[2 * i + f // 2][:, f % 2, :], w1[i][:, f * P:(f + 1) * P], xeT[i][:, :],
                                           start=True, stop=True)
                    if f % 2:
                        ins.then_inc(h_done, 1)

            def second(it, i):
                n = it * NW + i
                pe.wait_ge(relu_act, n + 3)
                pe.wait_ge(relu_dve, n + 3)
                pe.wait_ge(w2_ready[i], (it + 1) * 32)
                pe.wait_ge(ye_ready, n + 1)
                for c in range(2):
                    for f in range(FB):
                        ins = nc.tensor.matmul(y_ps[i][:, c, :], hT[i][:, f, c * P:(c + 1) * P], w2[i][:, f, :],
                                               start=f == 0, stop=f == FB - 1)
                ins.then_inc(y_done, 1)

            assert NW == 2
            turn(0, 0)
            turn(0, 1)
            first(0, 0)
            with pe.Fori(0, ITS - 1) as it:
                first(it, 1)
                turn(it + 1, 0)
                second(it, 0)
                first(it + 1, 0)
                turn(it + 1, 1)
                second(it, 1)
            first(ITS - 1, 1)
            second(ITS - 1, 0)
            second(ITS - 1, 1)

        @block.scalar
        def _(act):
            def body(it, last):
                for i in range(NW):
                    n = it * NW + i
                    act.wait_ge(turned, n + 1)
                    nc.scalar.activation(xeT[i][:, :], t_ps[i][:, :], ACT.Copy).then_inc(xeT_ready, 1)
                    act.wait_ge(h_done, 2 * n + 1)
                    for f in range(2):
                        ins = nc.scalar.activation(hT[i][:, f, :], h_ps[2 * (i % 2)][:, f, :], ACT.Relu,
                                                   bias=b1T[:, f, bass.ds(n, 1)])
                    ins.then_inc(relu_act, 1)
                    if not last:
                        act.wait_ge(h_done, 2 * n + 2)
                        first_layer(act, (it + 1) * NW + i, i)

            with act.Fori(0, ITS - 1) as it:
                body(it, False)
            body(ITS - 1, True)

        @block.vector
        def _(dve):
            def body(it):
                for i in range(NW):
                    n = it * NW + i
                    dve.wait_ge(h_done, 2 * n + 2)
                    for f in range(2, FB):
                        ins = nc.vector.tensor_scalar(hT[i][:, f, :], h_ps[2 * (i % 2) + 1][:, f % 2, :],
                                                      b1T[:, f, bass.ds(n, 1)], 0.0, ALU.add, ALU.max)
                    ins.then_inc(relu_dve, 1)
                    dve.wait_ge(w2_ready[i], (it + 1) * 32)
                    dve.wait_ge(y_done, n + 1)
                    dve.wait_ge(stored[i], (it + 1) * 16)
                    nc.vector.tensor_tensor(ye[i][:, :, :], y_ps[i][:, :, :],
                                            b2[i][:, :].unsqueeze(1).to_broadcast([P, 2, D]), ALU.add).then_inc(ye_ready, 1)

            with dve.Fori(0, ITS) as it:
                body(it)
            for i in range(TILES):
                if i % BLK == 0:
                    dve.wait_ge(fetched[i // BLK], 16 * BLK)
                nc.vector.scalar_tensor_tensor(X[:, i, :], back[:, i, :], gate[:, i:i + 1], X[:, i, :], ALU.mult, ALU.add)


def geometry(nc, xnT, w_geo, sel, row_decay, scale_row, kv_gate, gate, ident):
    H = B_HEADS
    with Phase(nc, "geo") as ph:
        G = ph.sb("G", [P, TILES, 4, H, 4])
        L, Ls = ph.sb("L", [P, TILES, 2, H, 9]), ph.sb("Ls", [P, TILES, 2, H, 9])
        T = ph.sb("T", [P, 6, TILES, 2 * H])
        nrm, inv = ph.sb("nrm", [P, TILES, 2 * H]), ph.sb("inv", [P, TILES, 2 * H])
        prod = [ph.sb(f"prod{w}", [P, TILES, PAIRS, H]) for w in range(2)]
        g_done, g_moved, chain, lines = ph.sem("g_done"), ph.sem("g_moved"), ph.sem("chain"), ph.sem("lines")
        made = [ph.sem(f"made{w}") for w in range(2)]
        turned, used = ph.sem("turned"), ph.sem("used")
        M = [ph.sb(f"M{i}", [ROWS, SEQ + 1]) for i in range(2)]
        RM = ph.sb("RM", [ROWS, 3, TOK])
        scanned, scored, nz, ez = ph.sem("scanned"), ph.sem("scored"), ph.sem("nz"), ph.sem("ez")
        bank = [ph.psum(f"bank{i}", [P, BANK]) for i in range(7)]
        s_ps = ph.psum("s", [P, TILES, H])
        z, e1 = ph.sb("z", [P, TILES, H]), ph.sb("e1", [P, TILES, H])
        decay_b = row_decay[0:ROWS, 0:1].to_broadcast([ROWS, SEQ])
        block = ph.block()
        LINE = ((0, 1), (0, 2), (0, 3), (2, 3), (1, 3), (1, 2))
        minus, scaled = ph.sem("minus"), ph.sem("scaled")

        def pt(a, c):
            return G[:, :, 2 * a:2 * a + 2, :, c].rearrange("p t w h -> p t (w h)")

        def products(eng, w):
            o, n = 3 * w, 0
            for a in range(6):
                k = 6 - a
                ins = eng.tensor_tensor(
                    prod[w][:, :, n:n + k, :].rearrange("p t a h -> p t h a"),
                    L[:, :, w, :, o + a:o + a + 1].to_broadcast([P, TILES, H, k]),
                    Ls[:, :, w, :, o + a:o + 6], ALU.mult)
                n += k
            ins.then_inc(made[w], 1)

        @block.gpsimd
        def _(pool):
            pool.wait_ge(g_moved, TILES // 2)
            for c, (i, j) in enumerate(LINE):
                nc.gpsimd.tensor_tensor(T[:, c, :, :], pt(0, j), pt(1, i), ALU.mult).then_inc(minus, 1)
            pool.wait_ge(scaled, 1)
            products(nc.gpsimd, 1)

        order = [(b, g, w, c) for b in range(BATCH) for g in range(3) for w in range(2) for c in range(2)]

        @block.tensor
        def _(pe):
            for i in range(TILES):
                at, b, o = (i % QT) * P, i // QT, (i % 2) * 4 * H * 4
                if i % 2 == 0 and i // 2 >= 7:
                    pe.wait_ge(g_moved, i // 2 - 6)
                out = bank[(i // 2) % 7]
                nc.tensor.matmul(out[:, o:o + 64], xnT[:, b, at:at + P], w_geo[:, 0:64], start=True, stop=True)
                ins = nc.tensor.matmul(out[:, o + 64:o + 256], xnT[:, b, 1 + at:1 + at + P], w_geo[:, 64:256], start=True, stop=True)
                if i % 2:
                    ins.then_inc(g_done, 1)
            for n, (b, g, w, c) in enumerate(order):
                if (b, g, c) == (0, 0, 0):
                    pe.wait_ge(made[w], 1)
                if n < 7:
                    pe.wait_ge(g_moved, 8)
                else:
                    pe.wait_ge(used, n - 6)
                for j in range(BLK):
                    ins = nc.tensor.transpose(bank[n % 7][0:ROWS, j * P:(j + 1) * P],
                                              prod[w][:, b * QT + c * BLK + j, 7 * g:7 * g + 7, :].rearrange("p a h -> p (a h)"),
                                              ident[:, :])
                ins.then_inc(turned, 1)
            for i in range(TILES):
                if i % BLK == 0:
                    pe.wait_ge(used, len(order) * (i // QT + 1) // BATCH - (1 - i % QT // BLK))
                for g in range(3):
                    ins = nc.tensor.matmul(s_ps[:, i, :], RM[:, g, i * P:(i + 1) * P], sel[0:ROWS, g, :],
                                           start=g == 0, stop=g == 2)
            ins.then_inc(scored, 1)

        @block.scalar
        def _(act):
            for i in range(TILES // 2):
                act.wait_ge(g_done, i + 1)
                nc.scalar.activation(G[:, 2 * i:2 * i + 2, :, :, :].rearrange("p t a h c -> p (t a h c)"), bank[i % 7][:, :],
                                     ACT.Copy).then_inc(g_moved, 1)
            act.wait_ge(nz, 1)
            nc.scalar.activation(e1[:, :, :], z[:, :, :], ACT.Exp, scale=-1.0).then_inc(ez, 1)

        @block.vector
        def _(dve):
            link = Chain(dve, chain)
            dve.wait_ge(g_moved, TILES // 2)

            def line(src, c):
                return src[:, :, :, :, c].rearrange("p t w h -> p t (w h)")

            for c, (i, j) in enumerate(LINE):
                ins = nc.vector.tensor_tensor(line(L, c), pt(0, i), pt(1, j), ALU.mult)
            link(ins)
            dve.wait_ge(minus, 6)
            for c in range(6):
                ins = nc.vector.tensor_tensor(line(L, c), line(L, c), T[:, c, :, :], ALU.subtract)
            link(ins)
            link(nc.vector.tensor_copy(L[:, :, :, :, 6:9].rearrange("p t w h c -> p (t w h) c"),
                                       L[:, :, :, :, 0:3].rearrange("p t w h c -> p (t w h) c")))
            flat = [x[:, :, :, :, :].rearrange("p t w h c -> p (t w h) c") for x in (L, Ls)]
            link(nc.vector.tensor_tensor(flat[1], flat[0], flat[0], ALU.mult))
            nflat, iflat = (x[:, :, :].rearrange("p t w -> p (t w)") for x in (nrm, inv))
            link(nc.vector.tensor_reduce(nflat, flat[1][:, :, 0:6], AX.X, ALU.add))
            link(nc.vector.tensor_scalar(nflat, nflat, 1e-24, None, ALU.max))
            link(nc.vector.reciprocal(iflat, nflat))
            link(nc.vector.tensor_tensor(flat[1], flat[0], iflat.unsqueeze(2).to_broadcast([P, TILES * 2 * H, 9]), ALU.mult))
            dve.sem_inc(scaled, 1)
            products(nc.vector, 0)
            for i in range(2):
                link(nc.vector.memset(M[i][:, 0:1], 0.0))
            for b in range(BATCH):
                for g in range(3):
                    n = (b * 3 + g) * 4
                    m = M[g % 2]
                    for c in range(2):
                        dve.wait_ge(turned, n + c + 1)
                        nc.vector.tensor_tensor_scan(m[:, 1 + c * BANK:1 + (c + 1) * BANK], decay_b[:, 0:BANK],
                                                     bank[(n + c) % 7][0:ROWS, :],
                                                     0.0 if c == 0 else m[:, c * BANK:c * BANK + 1],
                                                     ALU.mult, ALU.add).then_inc(used, 1)
                        dve.wait_ge(used, n + c + 1)
                    for c in range(2):
                        dve.wait_ge(turned, n + c + 3)
                        ins = nc.vector.scalar_tensor_tensor(RM[:, g, b * SEQ + c * BANK:b * SEQ + (c + 1) * BANK],
                                                             bank[(n + 2 + c) % 7][0:ROWS, :], row_decay[0:ROWS, 0:1],
                                                             m[:, c * BANK:(c + 1) * BANK], ALU.mult, ALU.mult)
                        ins.then_inc(used, 1)
                        dve.wait_ge(used, n + c + 3)
            dve.wait_ge(scored, 1)
            nc.vector.tensor_tensor(z[:, :, :], s_ps[:, :, :], scale_row[:, :].unsqueeze(1).to_broadcast([P, TILES, H]),
                                    ALU.mult).then_inc(nz, 1)
            dve.wait_ge(ez, 1)
            link(nc.vector.tensor_scalar(e1[:, :, :], e1[:, :, :], 1.0, None, ALU.add))
            link(nc.vector.reciprocal(z[:, :, :], e1[:, :, :]))
            nc.vector.tensor_scalar(gate[:, :, :], z[:, :, :], kv_gate[:, 0:1], None, ALU.mult)


def prepare_b(nc, xnT, w_kv, kv_bias, w_q, q_bias, gate, QS4, KS4, Vb, hi_sign, lo_q, lo_k, ident):
    H = B_HEADS
    NG = H // GRP
    with Phase(nc, "prep_b") as ph:
        kv = ph.sb("kv", [P, TILES, 4, H, B_DH])
        rep = [ph.sb(f"rep{i}", [P, NG, GRP, REP, B_DH]) for i in range(2)]
        q = [ph.sb(f"q{i}", [P, BANK]) for i in range(4)]
        kv_ps = [ph.psum(f"kvp{i}", [P, BANK]) for i in range(2)]
        k_ps = [ph.psum(f"kp{i}", [P, BANK]) for i in range(2)]
        q_ps = [ph.psum(f"qp{i}", [P, BANK]) for i in range(2)]
        kv_done, kv_read, rep_done = ph.sem("kv_done"), ph.sem("kv_read"), ph.sem("rep_done")
        k_done, k_high, k_free = ph.sem("k_done"), ph.sem("k_high"), ph.sem("k_free")
        q_shift = ph.sb("q_shift", [P, NG])
        shifted, pool_chain, keyed = ph.sem("shifted"), ph.sem("pool_chain"), ph.sem("keyed")
        q_done, q_copied, q_high, q_low = ph.sem("q_done"), ph.sem("q_copied"), ph.sem("q_high"), ph.sem("q_low")
        block = ph.block()
        LAG = 3

        @block.tensor
        def _(pe):
            def keys(i):
                pe.wait_ge(rep_done, i + 1)
                if i >= 2:
                    pe.wait_ge(k_free, i - 1)
                for g in range(NG):
                    ins = nc.tensor.transpose(k_ps[i % 2][:, g * P:(g + 1) * P],
                                              rep[i % 2][:, g, :, :, :].rearrange("p a r d -> p (a r d)"), ident[:, :])
                ins.then_inc(k_done, 1)

            for i in range(TILES):
                at, b = 1 + (i % QT) * P, i // QT
                if i >= 2:
                    pe.wait_ge(kv_read, i - 1)
                nc.tensor.matmul(kv_ps[i % 2][:, :], xnT[:, b, at:at + P], w_kv[:, :], start=True, stop=True).then_inc(kv_done, 1)
                g, t = i // 4, i % 4
                if i >= 2:
                    pe.wait_ge(q_copied, i - 1)
                nc.tensor.matmul(q_ps[i % 2][:, :], w_q[:, g, :], xnT[:, t // 2, 1 + (t % 2) * BANK:1 + (t % 2 + 1) * BANK],
                                 start=True, stop=True).then_inc(q_done, 1)
                if i >= 2:
                    keys(i - 2)
            keys(TILES - 2)
            keys(TILES - 1)

        @block.scalar
        def _(act):
            def high_keys(i):
                act.wait_ge(k_done, i + 1)
                nc.scalar.activation(KS4[:, :, i * P:(i + 1) * P], k_ps[i % 2][:, :].rearrange("p (g t) -> p g t", g=NG),
                                     ACT.Copy, scale=hi_sign[:, 1:2]).then_inc(k_high, 1)

            act.wait_ge(shifted, 1)
            for i in range(TILES):
                g, t = i // 4, i % 4
                act.wait_ge(q_done, i + 1)
                if i >= 4:
                    act.wait_ge(q_low, i - 3)
                nc.scalar.activation(q[i % 4][:, :], q_ps[i % 2][:, :], ACT.Identity, bias=q_shift[:, g:g + 1],
                                     scale=-(B_DH ** -0.5)).then_inc(q_copied, 1)
                act.wait_ge(q_copied, i + 1)
                nc.scalar.activation(QS4[:, g, t * BANK:(t + 1) * BANK], q[i % 4][:, :], ACT.Copy, scale=hi_sign[:, 0:1]).then_inc(q_high, 1)
                if i >= 2:
                    high_keys(i - 2)
            for i in range(TILES - 2, TILES):
                high_keys(i)

        @block.vector
        def _(dve):
            nc.vector.tensor_scalar(q_shift[:, :], q_bias[:, :], -(B_DH ** -0.5), None, ALU.mult).then_inc(shifted, 1)

            def repeat(i):
                dve.wait_ge(keyed, i + 1)
                if i >= 2:
                    dve.wait_ge(k_done, i - 1)
                nc.vector.tensor_copy(rep[i % 2][:, :, :, :, :].rearrange("p g a r d -> p (g a) r d"),
                                      kv[:, i, 0, :, :].unsqueeze(2).to_broadcast([P, H, REP, B_DH])).then_inc(rep_done, 1)

            def low(i):
                g, t = i // 4, i % 4
                dve.wait_ge(q_high, i + 1)
                dst = QS4[:, g, t * BANK:(t + 1) * BANK]
                nc.vector.scalar_tensor_tensor(dst, q[i % 4][:, :], lo_q, dst.bitcast(F32), ALU.mult, ALU.add).then_inc(q_low, 1)
                dve.wait_ge(k_high, i + 1)
                dst = KS4[:, :, i * P:(i + 1) * P]
                nc.vector.scalar_tensor_tensor(dst, k_ps[i % 2][:, :].rearrange("p (g t) -> p g t", g=NG), lo_k,
                                               dst.bitcast(F32), ALU.mult, ALU.add).then_inc(k_free, 1)

            for i in range(TILES):
                dve.wait_ge(kv_done, i + 1)
                nc.vector.tensor_tensor(kv[:, i, :, :, :].rearrange("p a h d -> p (a h d)"), kv_ps[i % 2][:, :],
                                        kv_bias[:, :], ALU.add).then_inc(kv_read, 1)
                if i >= 1:
                    repeat(i - 1)
                if i >= LAG:
                    low(i - LAG)
            repeat(TILES - 1)
            for i in range(TILES - LAG, TILES):
                low(i)

        @block.gpsimd
        def _(pool):
            link = Chain(pool, pool_chain)
            for i in range(TILES):
                pool.wait_ge(kv_read, i + 1)
                for a in range(2):
                    geo = kv[:, i, 2 + a, :, :]
                    ins = nc.gpsimd.tensor_tensor(geo, geo, gate[:, i, :].unsqueeze(2).to_broadcast([P, H, B_DH]), ALU.mult)
                link(ins)
                nc.gpsimd.tensor_tensor(kv[:, i, 0, :, :], kv[:, i, 0, :, :], kv[:, i, 2, :, :], ALU.add).then_inc(keyed, 1)
                nc.gpsimd.tensor_tensor(Vb[:, i, :].rearrange("p (h d) -> p h d", h=H), kv[:, i, 1, :, :], kv[:, i, 3, :, :], ALU.add)


COLS, at = {}, 0
for key, width in (("ident", P), ("upper", P), ("ones", P), ("window", P), ("prio", TILES * E), ("ebase", TILES * E),
                   ("spare", TILES), ("sel", 3 * B_HEADS), ("hmask", GRP), ("sign", 2), ("low", 2), ("bucket", BIAS_M)):
    COLS[key] = (at, at + width)
    at += width
TABLE_W = at


def tables():
    t = np.zeros((P, TABLE_W), np.float32)

    def put(key, a):
        lo, hi = COLS[key]
        t[:a.shape[0], lo:hi] = a

    r = np.arange(P)
    put("ident", np.eye(P))
    put("upper", r[:, None] <= r[None, :])
    put("ones", np.ones((P, P)))
    put("window", np.where(r[None, :] > r[:, None], MASKED, 0.0))
    put("prio", np.tile(E - np.arange(E), (P, TILES)))
    put("ebase", np.tile(CAP * np.arange(E), (P, TILES)))
    put("spare", SLOTS + 1 + P * np.arange(TILES)[None, :] + r[:, None])
    pairs = [(a, b) for a in range(6) for b in range(a, 6)]
    sign = [1, -1, 1, 1, -1, 1]
    sel = np.zeros((ROWS, 3, B_HEADS))
    for n, (a, b) in enumerate(pairs):
        for h in range(B_HEADS):
            sel[(n % 7) * B_HEADS + h, n // 7, h] = sign[a] * sign[b] * (1 if a == b else 2)
    put("sel", sel.reshape(ROWS, -1))
    copy = (r // B_DH) % REP
    put("hmask", (r[:, None] // (P // GRP)) == np.arange(GRP)[None, :])
    low = np.stack([copy % 2, copy // 2], 1)
    put("sign", 1.0 - 2.0 * low)
    put("low", low)
    bucket = np.zeros((BUCKETS + 1, BIAS_M), np.float32)
    for m in range(BIAS_M):
        n = 2 * P - 1 - m
        if n < 0:
            bucket[BUCKETS, m] = MASKED
            continue
        half = BUCKETS // 2
        which = n
        if n >= half:
            which = min(half + int(np.log(np.float32(n) / half) / np.log(MAX_DIST / half) * (BUCKETS - half)), BUCKETS - 1)
        bucket[which, m] -= A_DH ** 0.5
        bucket[BUCKETS - 1, m] += A_DH ** 0.5
    put("bucket", bucket)
    return t


def build(nc, t, out):
    ctx = ExitStack()
    with ctx:
        def sb(name, shape, dt=F32):
            return ctx.enter_context(nc.sbuf_tensor(name, shape, dt))

        def dram(name, shape):
            return nc.dram_tensor(name, shape, F32, kind="Internal")

        X, xn, xnT = sb("X", [P, TILES, D]), sb("xn", [P, TILES, D]), sb("xnT", [P, BATCH, SEQ + 1])
        tab = sb("tab", [P, TABLE_W])
        col = {k: tab[:, lo:hi] for k, (lo, hi) in COLS.items()}
        ident = col["ident"]
        upper_bf, ones_bf = sb("upper_bf", [P, P], BF16), sb("ones_bf", [P, P], BF16)
        wkv = sb("wkv", [P, 2, 2, A_DH])
        woa, bouta = sb("woa", [P, A_HEADS * A_DH // P, D]), sb("bouta", [P, D])
        router, b1T = sb("router", [P, E]), sb("b1T", [P, FB, E])
        w_geo, qkvw, geow = sb("w_geo", [P, 4, 4 * B_HEADS]), sb("qkvw", [P, 3 * D]), sb("geow", [P, 2 * D])
        w_kv, w_q = sb("w_kv", [P, BANK]), sb("w_q", [P, B_HEADS // GRP, P])
        kv_bias, q_bias = sb("kv_bias", [P, BANK]), sb("q_bias", [P, B_HEADS // GRP])
        wob, boutb = sb("wob", [P, 1, D]), sb("boutb", [P, D])
        kv_gate, scale_row, decay = sb("kv_gate", [P, 1]), sb("scale_row", [P, B_HEADS]), sb("decay", [P, 1])
        slot, gate = sb("slot", [P, TILES], I32), sb("gate", [P, TILES])
        bias_dram = dram("bias_by_query_and_key", [A_HEADS * P, BIAS_W])
        by_dist_dram, xe_dram, ye_dram = dram("bias_by_distance", [B_HEADS, BIAS_M]), dram("to_experts", [SLOTS + TOK, D]), dram("from_experts", [SLOTS + TOK, D])

        def row(a, n, offset=0):
            return bass.AP(tensor=a.tensor, offset=offset, ap=[[0, P], [1, n]])

        with Phase(nc, "setup") as ph:
            rel = ph.sb("rel", [BUCKETS + 1, A_HEADS])
            g_sb = ph.sb("g_sb", [A_HEADS, BIAS_M])
            zero = ph.sb("zero", [P, TILES, D])
            g_ps = ph.psum("g", [P, BANK])
            loaded, one_row, g_done, g_ready, zeroed = (ph.sem(n) for n in ("loaded", "one_row", "g_done", "g_ready", "zeroed"))
            g_stored, decays, zfill, late = ph.sem("g_stored"), ph.sem("decays"), ph.sem("zfill"), ph.sem("late")
            dec_in, dec_e = ph.sb("dec_in", [P, 1]), ph.sb("dec_e", [P, 1])
            block = ph.block()
            LATE = 1 + 12 + 4

            @block.sync
            def _(sp):
                sp.dma_start(X[:, :, :], t["x"].rearrange("b (t p) d -> p (b t) d", p=P)).then_inc(late, 16)
                sp.dma_start(tab[:, :], t["table"]).then_inc(loaded, 16)
                sp.dma_start(rel[0:BUCKETS, :], t["rel_emb"]).then_inc(loaded, 16)
                for dst, src in (
                    [(wkv[:, 0, :, :], bass.AP(tensor=t["Wkv"].tensor, offset=0, ap=[[2 * A_DH, P], [0, 2], [1, A_DH]])),
                     (wkv[:, 1, :, :], bass.AP(tensor=t["Wkv"].tensor, offset=A_DH, ap=[[2 * A_DH, P], [0, 2], [1, A_DH]])),
                     (woa[:, :, :], t["Wout"].rearrange("(j p) d -> p j d", p=P)), (bouta[:, :], row(t["bout"], D)),
                     (router[:, :], t["router_w"]), (qkvw[:, :], t["qkv_w"]), (geow[:, :], t["kv_geo_w"]),
                     (kv_bias[:, 0:2 * D], row(t["qkv_b"], 2 * D, D)), (wob[:, 0, :], t["out_w"]), (boutb[:, :], row(t["out_b"], D)),
                     (kv_gate[:, :], bass.AP(tensor=t["kv_gate"].tensor, offset=0, ap=[[0, P], [1, 1]])),
                     (scale_row[:, :], row(t["mem_scale"], B_HEADS))]
                    + [(w_geo[:, i, :], t[k]) for i, k in enumerate(("w1_write", "w1_read", "w2_write", "w2_read"))]
                ):
                    sp.dma_start(dst, src).then_inc(late, 16)
                sp.wait_ge(zeroed, 2)
                sp.dma_start(bass.AP(tensor=xe_dram, offset=0, ap=[[D, P], [P * D, TILES], [1, D]]), zero[:, :, :]).then_inc(zfill, 16)
                sp.dma_start(bass.AP(tensor=ye_dram, offset=SLOTS * D, ap=[[D, P], [P * D, TILES], [1, D]]), zero[:, :, :]).then_inc(zfill, 16)
                sp.wait_ge(g_ready, 1)
                sp.dma_start(by_dist_dram[:, :], g_sb[:, :]).then_inc(g_stored, 16)
                sp.wait_ge(g_stored, 16)
                sp.dma_start(bias_dram[:, :].rearrange("(h p) w -> h p w", p=P),
                             bass.AP(tensor=by_dist_dram, offset=P - 1, ap=[[BIAS_M, A_HEADS], [-1, P], [1, BIAS_W]])
                             ).then_inc(g_stored, 16)
                sp.wait_ge(g_stored, 32)
                sp.wait_ge(zfill, 32)
                sp.wait_ge(late, 16 * LATE)

            @block.scalar
            def _(act):
                for h in range(ROWS // B_HEADS):
                    act.dma_start(dec_in[h * B_HEADS:(h + 1) * B_HEADS, :], t["decay_logits"].rearrange("(h a) -> h a", a=1)).then_inc(decays, 16)
                for a in range(GRP):
                    for r in range(REP):
                        act.dma_start(q_bias[a * 32 + r * B_DH:a * 32 + (r + 1) * B_DH, :],
                                      bass.AP(tensor=t["qkv_b"].tensor, offset=a * B_DH, ap=[[1, B_DH], [GRP * B_DH, B_HEADS // GRP]]), allow_slow_non_contiguous=True
                                      ).then_inc(one_row, 16)
                for f in range(FB):
                    act.dma_start(b1T[:, f, :], t["b1"][:, f * P:(f + 1) * P].rearrange("e p -> p e"), allow_slow_non_contiguous=True).then_inc(one_row, 16)
                act.wait_ge(decays, 16 * (ROWS // B_HEADS))
                nc.scalar.activation(dec_e[0:ROWS, :], dec_in[0:ROWS, :], ACT.Exp, scale=-1.0).then_inc(decays, 1)
                act.wait_ge(one_row, 16 * (GRP * REP + FB))

            @block.tensor
            def _(pe):
                pe.wait_ge(loaded, 32)
                pe.wait_ge(zeroed, 2)
                lo, hi = COLS["bucket"]
                nc.tensor.matmul(g_ps[0:A_HEADS, 0:BIAS_M], rel[:, :], tab[0:BUCKETS + 1, lo:hi], start=True, stop=True).then_inc(g_done, 1)

            @block.vector
            def _(dve):
                nc.vector.memset(rel[BUCKETS:BUCKETS + 1, :], 1.0).then_inc(zeroed, 1)
                nc.vector.memset(zero[:, :, :], 0.0).then_inc(zeroed, 1)
                nc.vector.memset(kv_bias[:, 2 * D:], 0.0)
                dve.wait_ge(g_done, 1)
                nc.vector.tensor_copy(g_sb[:, :], g_ps[0:A_HEADS, 0:BIAS_M]).then_inc(g_ready, 1)
                nc.vector.tensor_copy(upper_bf[:, :], col["upper"])
                nc.vector.tensor_copy(ones_bf[:, :], col["ones"])
                dve.wait_ge(decays, 16 * (ROWS // B_HEADS) + 1)
                nc.vector.tensor_scalar(dec_e[0:ROWS, :], dec_e[0:ROWS, :], 1.0, None, ALU.add).then_inc(g_ready, 1)
                dve.wait_ge(g_ready, 2)
                nc.vector.reciprocal(decay[0:ROWS, :], dec_e[0:ROWS, :])

            @block.gpsimd
            def _(pool):
                pool.wait_ge(late, 16 * LATE)
                nc.gpsimd.tensor_copy(w_kv[:, 0:2 * D], qkvw[:, D:])
                nc.gpsimd.tensor_copy(w_kv[:, 2 * D:], geow[:, :])
                nc.gpsimd.tensor_copy(w_q[:, :, :].rearrange("p g (a r d) -> p (g a) r d", a=GRP, r=REP),
                                      qkvw[:, 0:D].rearrange("p (h d) -> p h d", h=B_HEADS).unsqueeze(2).to_broadcast([P, B_HEADS, REP, B_DH]))

        def moe(name):
            with nc.psum_tensor(name + "_logit", [P, BANK // E, E], F32) as banked:
                logit = banked[:, 0:TILES, :]
                layernorm(nc, name + "_ln", X, xn, xnT, ident, router, logit)
                route(nc, name + "_route", logit,
                      (upper_bf, ones_bf) + tuple(col[k].rearrange("p (t e) -> p t e", t=TILES) for k in ("prio", "ebase"))
                      + (col["spare"],), slot, gate)
            experts(nc, name + "_experts", xn, X, slot, gate, b1T, t["b2"], t["w1"], t["w2"], xe_dram, ye_dram, ident)

        layernorm(nc, "a_ln", X, xn, xnT, ident)
        with ExitStack() as a:
            KH, KL = (a.enter_context(nc.sbuf_tensor(n, [P, TOK], F32R)) for n in ("KH", "KL"))
            Vd = a.enter_context(nc.sbuf_tensor("Vd", [P, TILES, P], F32))
            O = a.enter_context(nc.sbuf_tensor("O", [P, TILES, A_HEADS * A_DH], F32))
            QS = [a.enter_context(nc.sbuf_tensor(f"QSa{i}", [P, SEQ], F32R)) for i in range(4)]
            prepare_a(nc, xnT, wkv[:, :, :, :].rearrange("p a b d -> p a (b d)"), KH, KL, Vd)
            attention(nc, "attn_a", True, 4, (KH, KL), Vd, O, QS, ident, None, xnT, t["Wq"], bias_dram, None, None)
            project_out(nc, "out_a", O, A_HEADS * A_DH // P, woa, bouta, X, ident)
        moe("moe1")
        layernorm(nc, "b_ln", X, xn, xnT, ident)
        with ExitStack() as a:
            gate_b = a.enter_context(nc.sbuf_tensor("gate_b", [P, TILES, B_HEADS], F32))
            geometry(nc, xnT, w_geo[:, :, :].rearrange("p a b -> p (a b)"), col["sel"].rearrange("p (g h) -> p g h", g=3),
                     decay, scale_row, kv_gate, gate_b, ident)
            QS4, KS4 = (a.enter_context(nc.sbuf_tensor(n, [P, B_HEADS // GRP, TOK], F32R)) for n in ("QS4", "KS4"))
            Vb = a.enter_context(nc.sbuf_tensor("Vb", [P, TILES, D], F32))
            O = a.enter_context(nc.sbuf_tensor("Ob", [P, TILES, D], F32))
            lo = COLS["low"][0]
            prepare_b(nc, xnT, w_kv, kv_bias, w_q, q_bias, gate_b, QS4, KS4, Vb, col["sign"],
                      tab[:, lo:lo + 1], tab[:, lo + 1:lo + 2], ident)
            QS = [a.enter_context(nc.sbuf_tensor(f"QSb{i}", [P, SEQ], F32R)) for i in range(2)]
            attention(nc, "attn_b", False, GRP, (KS4,), Vb, O, QS, ident, col["window"], None, None, None, QS4, col["hmask"])
            project_out(nc, "out_b", O, 1, wob, boutb, X, ident)
        moe("moe2")
        with Phase(nc, "store") as ph:
            stored = ph.sem("stored")
            block = ph.block()

            @block.sync
            def _(sp):
                sp.dma_start(out.rearrange("b (t p) d -> p (b t) d", p=P), X[:, :, :]).then_inc(stored, 16)
                sp.wait_ge(stored, 16)


def kernel(**inputs):
    import concourse.bacc as bacc
    from concourse.bass_utils import run_bass_kernel_spmd

    nc = bacc.Bacc("TRN2", target_bir_lowering=False, num_devices=1)
    arrays, args = {}, {}
    for name, a in list(inputs.items()) + [("table", tables())]:
        a = np.ascontiguousarray(a).reshape(np.shape(a) or (1,))
        key = f"in_{name}_dram"
        arrays[key] = a
        short = name
        for prefix in ("L0_attn_a_", "L0_attn_b_", "L0_ffn_"):
            short = short.removeprefix(prefix)
        args[short] = nc.dram_tensor(key, a.shape, mybir.dt.from_np(a.dtype), kind="ExternalInput").ap()
    out = nc.dram_tensor("out_0_dram", (BATCH, SEQ, D), F32, kind="ExternalOutput").ap()
    build(nc, args, out)
    r = run_bass_kernel_spmd(nc, [arrays], core_ids=[0])
    return r.results[0]["out_0_dram"]
```
